# Optimizing a Trainium2 kernel written in Bass

```python
import numpy as np
import jax
import jax.numpy as jnp

def _softmax(x, axis=-1):
    return jax.nn.softmax(x, axis=axis)

def _gelu(x):
    return jax.nn.gelu(x, approximate=True)

def _silu(x):
    return jax.nn.silu(x)

def _sigmoid(x):
    return jax.nn.sigmoid(x)

def _layernorm(x, axis=-1, eps=1e-05):
    m = jnp.mean(x, axis=axis, keepdims=True)
    v = jnp.var(x, axis=axis, keepdims=True)
    return (x - m) / jnp.sqrt(v + eps)

def _scatter_add(tgt, idx, src, axis=0):
    return tgt.at[idx].add(src)

def _segment_sum(src, seg, n):
    return jax.ops.segment_sum(src, seg, n)
kernel_name = 'mk_gnn_resnorm_d1_gnn_r8_bcbf58'

def setup_inputs(seed: int=0):
    np.random.seed(seed)
    _w = jnp.asarray

    def _rec_inputs():
        import jax
        import jax.numpy as jnp
        _gk = jax.random.key(seed)
        x = -0.000202 + 1 * jax.random.normal(jax.random.fold_in(_gk, 1), (6250, 128), jnp.float32)
        src = jax.random.randint(jax.random.fold_in(_gk, 2), (200000,), 0, 6250, jnp.int32)
        dst = jnp.minimum((6250 * jax.random.uniform(jax.random.fold_in(_gk, 3), (200000,)) ** 2.0).astype(jnp.int32), 49999)
        _o = jnp.argsort(dst, stable=True)
        src = src[_o]
        dst = dst[_o]
        edge_attr_128 = -5.16925e-05 + 1.00005 * jax.random.normal(jax.random.fold_in(_gk, 11), (200000, 128), jnp.float32)
        return (x, src, dst, edge_attr_128)
    x, src, dst, edge_attr_128 = _rec_inputs()

    def _L0_gnn_setup():
        import jax, jax.numpy as jnp
        import numpy as np
        N = 6250
        E = 100000
        D = 128
        DE = 128
        L = 3
        key = jax.random.key(seed)
        ks = jax.random.split(key, 10)
        s = 0.05
        return dict(x=jax.random.normal(ks[0], (N, D), jnp.float32), edge_index=jax.random.randint(ks[1], (2, E), 0, N, jnp.int32), edge_attr=jax.random.normal(ks[2], (E, DE), jnp.float32), W=jax.random.normal(ks[3], (L, D, D), jnp.float32) * s, att_src=jax.random.normal(ks[4], (L, D), jnp.float32) * s, att_dst=jax.random.normal(ks[5], (L, D), jnp.float32) * s, W_e=jax.random.normal(ks[6], (L, DE, D), jnp.float32) * s, att_edge=jax.random.normal(ks[7], (L, D), jnp.float32) * s, bias=jnp.zeros((L, D), jnp.float32), ln_gamma=jnp.ones((L, D), jnp.float32), ln_beta=jnp.zeros((L, D), jnp.float32))
    _L0_gnn_all = _L0_gnn_setup()
    _L0_gnn_in = {k: v for k, v in _L0_gnn_all.items() if k in ('W', 'att_src', 'att_dst', 'W_e', 'att_edge', 'bias', 'ln_gamma', 'ln_beta')}
    del _L0_gnn_all
    return {'x': x, 'src': src, 'dst': dst, 'edge_attr_128': edge_attr_128, 'L0_gnn_W': _L0_gnn_in['W'], 'L0_gnn_att_src': _L0_gnn_in['att_src'], 'L0_gnn_att_dst': _L0_gnn_in['att_dst'], 'L0_gnn_W_e': _L0_gnn_in['W_e'], 'L0_gnn_att_edge': _L0_gnn_in['att_edge'], 'L0_gnn_bias': _L0_gnn_in['bias'], 'L0_gnn_ln_gamma': _L0_gnn_in['ln_gamma'], 'L0_gnn_ln_beta': _L0_gnn_in['ln_beta']}

def reference(x, src, dst, edge_attr_128, L0_gnn_W, L0_gnn_att_src, L0_gnn_att_dst, L0_gnn_W_e, L0_gnn_att_edge, L0_gnn_bias, L0_gnn_ln_gamma, L0_gnn_ln_beta):
    import jax
    import jax.numpy as jnp

    def _L0_gnn_ref(x, edge_index, edge_attr, W, att_src, att_dst, W_e, att_edge, bias, ln_gamma, ln_beta):
        import jax, jax.numpy as jnp
        import numpy as np
        N = 6250
        E = 100000
        D = 128
        DE = 128
        L = 3
        n = x.shape[0]
        src, dst = (edge_index[0], edge_index[1])
        ones = jnp.ones((src.shape[0],), x.dtype)
        deg = jax.ops.segment_sum(ones, dst, num_segments=n)
        loop_attr = jax.ops.segment_sum(edge_attr, dst, num_segments=n) / jnp.maximum(deg, 1.0)[:, None]
        loop = jnp.arange(n, dtype=src.dtype)
        src_f = jnp.concatenate([src, loop])
        dst_f = jnp.concatenate([dst, loop])
        ea_f = jnp.concatenate([edge_attr, loop_attr], axis=0)

        def layer(h_in, p):
            Wl, asl, adl, Wel, ael, bl, gl, bel = p
            h = h_in @ Wl
            a = (h @ asl)[src_f] + (h @ adl)[dst_f] + ea_f @ (Wel @ ael)
            a = jnp.where(a > 0, a, 0.2 * a)
            m = jax.ops.segment_max(a, dst_f, num_segments=n)
            ea = jnp.exp(a - m[dst_f])
            denom = jax.ops.segment_sum(ea, dst_f, num_segments=n)
            alpha = ea / denom[dst_f]
            out = jax.ops.segment_sum(h[src_f] * alpha[:, None], dst_f, num_segments=n) + bl
            mu = jnp.mean(out, axis=-1, keepdims=True)
            var = jnp.var(out, axis=-1, keepdims=True)
            out = (out - mu) * jax.lax.rsqrt(var + 1e-05) * gl + bel
            return (out, None)
        h, _ = jax.lax.scan(layer, x, (W, att_src, att_dst, W_e, att_edge, bias, ln_gamma, ln_beta))
        return h
    edge_index = jnp.stack([src, dst])
    x = _layernorm(x + _L0_gnn_ref(x, edge_index, edge_attr_128, L0_gnn_W, L0_gnn_att_src, L0_gnn_att_dst, L0_gnn_W_e, L0_gnn_att_edge, L0_gnn_bias, L0_gnn_ln_gamma, L0_gnn_ln_beta), axis=-1)
    return x

_drawn_inputs = setup_inputs


def setup_inputs(seed=0):
    import zlib

    import numpy as np

    out = dict(_drawn_inputs(seed))
    spreads = {'L0_gnn_bias': (0.0, 0.1), 'L0_gnn_ln_gamma': (1.0, 0.2), 'L0_gnn_ln_beta': (0.0, 0.1)}
    factors = {'edge_attr_128': 3.713,
     'L0_gnn_att_dst': 51.869,
     'L0_gnn_W_e': 3.459,
     'L0_gnn_att_edge': 3.673}
    for name, (base, spread) in spreads.items():
        noise = np.random.default_rng([zlib.crc32(name.encode()), seed]).standard_normal(out[name].shape)
        drawn = base * np.exp(spread * noise) if base else spread * noise
        out[name] = jnp.asarray(drawn.astype(out[name].dtype))
    for name, factor in factors.items():
        out[name] = (out[name] * factor).astype(out[name].dtype)
    return out
```

```python
import numpy as np
import concourse.bass as bass
from concourse import mybir
from contextlib import ExitStack

FP32 = mybir.dt.float32
INT32 = mybir.dt.int32
BF16 = mybir.dt.bfloat16
ALU = mybir.AluOpType
ACT = mybir.ActivationFunctionType
AX = mybir.AxisListType

P = 128
N, E, D, L = 6250, 200000, 128, 3
NT = -(-N // P)
NCH = -(-E // P)
NVIS = NCH + NT - 1
NSB = -(-NVIS // 64)
NSB += NSB % 2
G = -(-NVIS // NSB)
G += G % 2
HG = G // 2
NV = NSB * G
BIG = 2.0 ** 100
LN_EPS = 1e-5
SLOPE = 0.2

C_ONE, C_S, C_M, C_T, C_CNT = D, D + 1, D + 1, D + 2, D + 2 + L
ROW = D + 2
SLOT = C_CNT + 1
S_RF, S_RB, S_OF, S_OB, S_RD, S_TI = 0, 1, 2, 3, 4, 5
NFIELD = 5 + L
EIW = P + 2 + P

KE = 16
ET = P * KE
NET = E // ET
REST = E - NET * ET
RK = next(k for k in range(1, KE + 1) if REST % k == 0 and REST // k <= P and (REST // k) % 16 == 0)
RP = REST // RK
SUB = 4
WXW = D + 3


class Chain:

    def __init__(self, eng, sem, base=0):
        self.eng, self.sem, self.base, self.n = eng, sem, base, 0

    def __call__(self, ins):
        self.n += 1
        ins.then_inc(self.sem, 1)
        self.eng.wait_ge(self.sem, self.base + self.n)


def build(nc, x, ei, chunk_last, edge_attr, w, wt, wet, att, params, out):
    table = nc.dram_tensor("table", (NT * P, ROW), FP32).ap()
    tnat = nc.dram_tensor("tnat", (NCH, L * P), FP32).ap()
    struct = nc.dram_tensor("struct", (NV, NFIELD * P), FP32).ap()
    perv = nc.dram_tensor("perv", (3, NV), FP32).ap()
    perv_i = nc.dram_tensor("perv_i", (1, NV), INT32).ap()

    ctx = ExitStack()

    def tensors(stack):
        def sb(name, shape, dt=FP32):
            return stack.enter_context(nc.sbuf_tensor(name, shape, dt))

        def ps(name):
            return stack.enter_context(nc.psum_tensor(name, [P, 512], FP32))

        def sem(name):
            return stack.enter_context(nc.semaphore(name))
        return sb, ps, sem

    with ctx:
        sb, ps_, sem = tensors(ctx)
        banks = [ps_(f"bank{i}") for i in range(8)]
        ident = sb("ident", [P, P])
        identb = sb("identb", [P, P], BF16)
        iota_row = sb("iota_row", [P, P])
        iota_col = sb("iota_col", [P, 1])
        ones_row = sb("ones_row", [1, P])
        idx = sb("idx", [P, NV], INT32)
        rdcol = sb("rdcol", [P, NV])
        carry_hot = sb("carry_hot", [P, NSB])
        carry_not = sb("carry_not", [P, NSB])
        ntile = sb("ntile", [1, NV], INT32)
        row_flags = sb("row_flags", [1, 2, NV])
        wx = sb("wx", [P, L, WXW])
        vcol = sb("vcol", [P, L])
        cvi = sb("cvi", [G, NSB], INT32)
        par = sb("par", [P, L, 3, P])

        with ExitStack() as st:
            sb, ps_, sem = tensors(st)
            cl = sb("cl", [P, NCH], INT32)
            clf = sb("clf", [P, NCH])
            vid = sb("vid", [G, NSB])
            ncol = sb("ncol", [P, 1])
            ndiag = sb("ndiag", [P, NT + 1])
            nrow = sb("nrow", [G, NT + 1])
            cmp = sb("cmp", [G, NSB, NT])
            nv = sb("nv", [G, NSB])
            n128 = sb("n128", [G, NSB])
            cvf = sb("cvf", [G, NSB])
            HS = NSB // 2
            eit = sb("eit", [G, HS, EIW], INT32)
            names = ["rd", "valid", "rf", "rb", "of", "ob", "tmp", "srcf"]
            a = {n: sb(f"a_{n}", [G, HS, P]) for n in names}
            r1 = sb("r1", [1, HS, P])
            r2 = sb("r2", [1, HS, P])
            cb = sb("cb", [1, NSB])
            pv = sb("pv", [NSB, 3, G])
            pvi = sb("pvi", [NSB, G], INT32)
            rowv = sb("rowv", [G, 3, NSB])
            clc = sb("clc", [P, NCH])
            attc = sb("attc", [P, 3 * L])
            wts = sb("wts", [P, 2, L, P])
            ones_g = sb("ones_g", [P, G])
            dst_loaded = sem("dst_loaded")
            weights_loaded = sem("weights_loaded")
            consts_made = sem("consts_made")
            ones_made = sem("ones_made")
            dve_chain = sem("dve_chain")
            tile_starts = sem("tile_starts")
            starts_spread = sem("starts_spread")
            chunks_known = sem("chunks_known")
            ints_gathered = sem("ints_gathered")
            masks_made = sem("masks_made")
            masks_stored = sem("masks_stored")
            columns_turned = sem("columns_turned")
            columns_kept = sem("columns_kept")
            half_used = sem("half_used")
            carry_found = sem("carry_found")
            carry_spread = sem("carry_spread")
            row_turned = sem("row_turned")
            row_made = sem("row_made")
            row_stored = sem("row_stored")
            row_back = sem("row_back")
            att_applied = sem("att_applied")
            with nc.Block() as block:
                NB = -(-HS // 8)

                @block.sync
                def _(sp):
                    sp.dma_start(cl[:, :], chunk_last.partition_broadcast(P)).then_inc(dst_loaded, 16)
                    sp.dma_start(attc[:, :], att).then_inc(weights_loaded, 16)
                    for l in range(L):
                        sp.dma_start(wx[:, l, 0:D], w[l]).then_inc(weights_loaded, 16)
                        sp.dma_start(wts[:, 0, l, :], wt[l]).then_inc(weights_loaded, 16)
                        sp.dma_start(wts[:, 1, l, :], wet[l]).then_inc(weights_loaded, 16)
                    sp.dma_start(par[:, :, :, :].rearrange("p l c d -> p (l c d)"),
                                 params.partition_broadcast(P)).then_inc(weights_loaded, 16)
                    for hh in range(2):
                        rows = struct[hh * HS * G:(hh + 1) * HS * G, :].rearrange("(s r) f -> r s f", r=G)
                        sp.wait_ge(masks_made, hh + 1)
                        for f, n in enumerate(["rf", "rb", "of", "ob", "rd"]):
                            sp.dma_start(rows[:, :, f * P:(f + 1) * P], a[n][:, :, :]).then_inc(masks_stored, 16)
                    sp.wait_ge(row_made, 1)
                    for f in range(2):
                        sp.dma_start(perv[f, :].rearrange("(s r) -> s r", r=G), pv[:, f + 1, :]).then_inc(row_stored, 16)
                    sp.dma_start(perv_i[0, :].rearrange("(s r) -> s r", r=G), pvi[:, :]).then_inc(row_stored, 16)
                    sp.wait_ge(row_stored, 48)
                    sp.dma_start(ntile[:, :], perv_i).then_inc(row_back, 16)
                    for f in range(2):
                        sp.dma_start(row_flags[:, f, :], perv[f:f + 1, :]).then_inc(row_back, 16)
                    sp.wait_ge(row_back, 48)
                    sp.wait_ge(masks_stored, 16 * 10)

                @block.gpsimd
                def _(pool):
                    nc.gpsimd.iota(iota_row[:, :], [[1, P]], base=0, channel_multiplier=0,
                                   allow_small_or_imprecise_dtypes=True).then_inc(consts_made, 1)
                    nc.gpsimd.iota(iota_col[:, :], [[1, 1]], base=0, channel_multiplier=1,
                                   allow_small_or_imprecise_dtypes=True).then_inc(consts_made, 1)
                    nc.gpsimd.iota(vid[:, :], [[G, NSB]], base=0, channel_multiplier=1,
                                   allow_small_or_imprecise_dtypes=True).then_inc(consts_made, 1)
                    nc.gpsimd.memset(ones_row[:, :], 1.0).then_inc(consts_made, 1)
                    nc.gpsimd.memset(ones_g[:, :], 1.0).then_inc(consts_made, 1)
                    nc.gpsimd.memset(ident[:, :], 0.0).then_inc(consts_made, 1)
                    pool.wait_ge(consts_made, 6)
                    nc.gpsimd.affine_select(out=ident[:, :], in_=ident[:, :], compare_op=ALU.not_equal, fill=1.0,
                                            base=0, pattern=[[-1, P]], channel_multiplier=1).then_inc(consts_made, 1)
                    pool.wait_ge(chunks_known, 1)
                    for hh in range(2):
                        if hh:
                            pool.wait_ge(half_used, 1)
                        for s in range(HS):
                            c = hh * HS + s
                            nc.gpsimd.indirect_dma_start(
                                eit[:, s, :], None, ei,
                                bass.IndirectOffsetOnAxis(cvi[:, c:c + 1], 0)).then_inc(ints_gathered, 16)

                @block.vector
                def _(dve):
                    v = nc.vector
                    link = Chain(dve, dve_chain)
                    dve.wait_ge(consts_made, 7)
                    link(v.tensor_copy(identb[:, :], ident[:, :]))
                    dve.wait_ge(dst_loaded, 16)
                    link(v.tensor_single_scalar(cl[:, :], cl[:, :], 7, ALU.arith_shift_right))
                    link(v.tensor_copy(clf[:, :], cl[:, :]))
                    link(v.tensor_scalar(clc[:, :], clf[:, :], iota_col[:, :], None, ALU.is_lt))
                    link(v.tensor_reduce(ncol[:, :], clc[:, :], AX.X, ALU.add))
                    link(v.tensor_scalar(ncol[:, :], ncol[:, :], float(NCH - 1), iota_col[:, :], ALU.min, ALU.add))
                    v.tensor_scalar(ndiag[:, :], ident[:, 0:NT + 1], ncol[:, :], None, ALU.mult).then_inc(tile_starts, 1)
                    dve.wait_ge(starts_spread, 1)
                    link(v.tensor_copy(nrow[:, :], banks[0][0:G, 0:NT + 1]))
                    link(v.tensor_tensor(cmp[:, :, :], vid[:, :].unsqueeze(2).broadcast_to([G, NSB, NT]),
                                         nrow[:, 1:NT + 1].unsqueeze(1).broadcast_to([G, NSB, NT]), ALU.is_ge))
                    link(v.tensor_reduce(nv[:, :], cmp[:, :, :], AX.X, ALU.add))
                    link(v.tensor_scalar(n128[:, :], nv[:, :], float(P), None, ALU.mult))
                    link(v.tensor_tensor(cvf[:, :], vid[:, :], nv[:, :], ALU.subtract))
                    link(v.tensor_scalar(rowv[:, 0, :], nv[:, :], float(NT - 1), None, ALU.min))
                    v.tensor_copy(cvi[:, :], cvf[:, :]).then_inc(chunks_known, 1)
                    for hh in range(2):
                        cols = slice(hh * HS, (hh + 1) * HS)
                        dve.wait_ge(ints_gathered, 16 * HS * (hh + 1))
                        if hh:
                            dve.wait_ge(masks_stored, 80)
                            dve.wait_ge(columns_turned, NB)
                        dst = eit[:, :, 1:P + 1]
                        link(v.tensor_tensor(a["rd"][:, :, :], dst,
                                             n128[:, cols].unsqueeze(2).broadcast_to([G, HS, P]), ALU.subtract))
                        link(v.tensor_scalar(a["tmp"][:, :, :], a["rd"][:, :, :], 0.0, None, ALU.is_ge))
                        link(v.scalar_tensor_tensor(a["valid"][:, :, :], a["rd"][:, :, :], float(P), a["tmp"][:, :, :],
                                                    ALU.is_lt, ALU.mult))
                        link(v.scalar_tensor_tensor(a["tmp"][:, :, :], a["rd"][:, :, :], 1.0, a["valid"][:, :, :],
                                                    ALU.add, ALU.mult))
                        link(v.tensor_scalar(a["rd"][:, :, :], a["tmp"][:, :, :], -1.0, None, ALU.add))
                        for n, off in (("rf", 0), ("rb", 2)):
                            link(v.tensor_tensor(a["tmp"][:, :, :], dst, eit[:, :, off:off + P], ALU.not_equal))
                            link(v.scalar_tensor_tensor(a[n][:, :, :], a["tmp"][:, :, :], -BIG, a["valid"][:, :, :],
                                                        ALU.mult, ALU.mult))
                        link(v.tensor_copy(a["srcf"][:, :, :], eit[:, :, P + 2:EIW]))
                        for s in range(HS):
                            v.tensor_tensor_scan(a["of"][:, s, :], a["rf"][:, s, :], a["rf"][:, s, :], 0.0,
                                                 ALU.min, ALU.min)
                            last = v.tensor_tensor_scan(a["ob"][:, s, ::-1], a["rb"][:, s, ::-1], a["rb"][:, s, ::-1],
                                                        0.0, ALU.min, ALU.min)
                        last.then_inc(masks_made, 1)
                        dve.wait_ge(masks_made, hh + 1)
                        link(v.tensor_copy(rowv[:, 1, cols], a["of"][:, :, P - 1]))
                        v.tensor_copy(rowv[:, 2, cols], a["ob"][:, :, 0]).then_inc(half_used, 1)
                        dve.wait_ge(half_used, hh + 1)
                        va = a["valid"][0:1, :, :]
                        link(v.tensor_tensor(r1[:, :, 1:P], va[:, :, 1:P], va[:, :, 0:P - 1], ALU.is_gt))
                        link(v.tensor_copy(r1[:, :, 0:1], va[:, :, 0:1]))
                        link(v.tensor_scalar(r2[:, :, :], a["rf"][0:1, :, :], 0.0, None, ALU.is_equal))
                        link(v.tensor_tensor(r1[:, :, :], r1[:, :, :], r2[:, :, :], ALU.mult))
                        link(v.scalar_tensor_tensor(r2[:, :, :], a["rd"][0:1, :, :], 1.0, r1[:, :, :], ALU.add, ALU.mult))
                        link(v.tensor_reduce(cb[:, cols], r2[:, :, :], AX.X, ALU.add))
                        for b in range(NB):
                            c0 = (hh * HS + b * 8) * G
                            c1 = (hh * HS + min(HS, b * 8 + 8)) * G
                            dve.wait_ge(columns_turned, hh * NB + b + 1)
                            v.tensor_copy(idx[:, c0:c1], banks[2 * b][:, 0:c1 - c0])
                            v.tensor_copy(rdcol[:, c0:c1], banks[2 * b + 1][:, 0:c1 - c0]).then_inc(columns_kept, 1)
                    v.tensor_scalar(cb[:, :], cb[:, :], -1.0, None, ALU.add).then_inc(carry_found, 1)
                    dve.wait_ge(carry_spread, 1)
                    v.tensor_scalar(carry_hot[:, :], banks[4][:, 0:NSB], iota_col[:, :], None, ALU.is_equal)
                    v.tensor_scalar(carry_not[:, :], banks[4][:, 0:NSB], iota_col[:, :], None, ALU.not_equal)
                    dve.wait_ge(row_turned, 1)
                    link(v.tensor_copy(pv[:, :, :], banks[5][0:NSB, 0:3 * G].rearrange("p (f g) -> p f g", f=3)))
                    v.tensor_copy(pvi[:, :], pv[:, 0, :]).then_inc(row_made, 1)
                    dve.wait_ge(weights_loaded, 16 * (3 * L + 2))
                    dve.wait_ge(att_applied, 1)
                    v.tensor_copy(wx[:, :, D + 1:D + 3], banks[6][:, 0:2 * L].rearrange("p (l c) -> p l c", c=2))
                    v.tensor_copy(vcol[:, :], banks[6][:, 2 * L:3 * L])
                    v.memset(wx[:, :, D:D + 1], 0.0)

                @block.tensor
                def _(pe):
                    t = nc.tensor
                    pe.wait_ge(tile_starts, 1)
                    t.matmul(banks[0][0:G, 0:NT + 1], ones_g[:, :], ndiag[:, :], start=True, stop=True)\
                        .then_inc(starts_spread, 1)
                    for hh in range(2):
                        pe.wait_ge(masks_made, hh + 1)
                        for b in range(NB):
                            if hh:
                                pe.wait_ge(columns_kept, b + 1)
                            for s in range(b * 8, min(HS, b * 8 + 8)):
                                o = (s - b * 8) * G
                                t.transpose(banks[2 * b][:, o:o + G], a["srcf"][:, s, :], ident[0:G, 0:G])
                                last = t.transpose(banks[2 * b + 1][:, o:o + G], a["rd"][:, s, :], ident[0:G, 0:G])
                            last.then_inc(columns_turned, 1)
                    pe.wait_ge(carry_found, 1)
                    t.matmul(banks[4][:, 0:NSB], ones_row[:, :], cb[:, :], start=True, stop=True).then_inc(carry_spread, 1)
                    for f in range(3):
                        last = t.transpose(banks[5][0:NSB, f * G:(f + 1) * G], rowv[:, f, :], ident[0:G, 0:G])
                    last.then_inc(row_turned, 1)
                    pe.wait_ge(weights_loaded, 16 * (3 * L + 2))
                    for l in range(L):
                        for j in range(3):
                            col = 2 * l + j if j < 2 else 2 * L + l
                            last = t.matmul(banks[6][:, col:col + 1], wts[:, j // 2, l, :],
                                            attc[:, 3 * l + j:3 * l + j + 1], start=True, stop=True)
                    last.then_inc(att_applied, 1)


        with ExitStack() as st:
            sb, ps_, sem = tensors(st)
            ea = sb("ea", [P, 2, KE, D])
            eat = sb("eat", [P, 2, SUB * P])
            trow = sb("trow", [L, 2, P, KE])
            tg = sb("tg", [G, NSB, L * P])
            rdr = sb("rdr", [G, NSB, P])
            invalid = sb("invalid", [G, NSB, P])
            ea_loaded = [sem("ea_loaded0"), sem("ea_loaded1")]
            turned = sem("turned")
            turned_kept = sem("turned_kept")
            t_made = sem("t_made")
            t_kept = sem("t_kept")
            t_stored = [sem("t_stored0"), sem("t_stored1")]
            rd_back = sem("rd_back")
            t_gathered = sem("t_gathered")
            mask_chain = sem("mask_chain")
            invalid_made = sem("invalid_made")
            t_masked = sem("t_masked")
            t_rows_stored = sem("t_rows_stored")
            tail_zeroed = sem("tail_zeroed")
            tv = tnat.rearrange("c (l e) -> l c e", l=L)
            RG = -(-RK // SUB)

            def groups(full):
                k = KE if full else RK
                return [(q, min(SUB, k - q)) for q in range(0, k, SUB)]
            NGRP = KE // SUB

            with nc.Block() as block:

                @block.sync
                def _(sp):
                    def load(tile, b, first=False):
                        if not first:
                            sp.wait_ge(turned, NGRP * (tile - 1))
                        sp.dma_start(ea[:, b, :, :].rearrange("p k d -> p (k d)"),
                                     edge_attr[bass.ds(tile * ET, ET), :].rearrange("(p k) d -> p (k d)", k=KE))\
                            .then_inc(ea_loaded[b], 16)
                    load(0, 0, True)
                    load(1, 1, True)
                    with sp.Fori(1, NET // 2) as i:
                        load(2 * i, 0)
                        load(2 * i + 1, 1)
                    load(NET - 1, 0)
                    sp.wait_ge(turned, NGRP * (NET - 1))
                    sp.dma_start(ea[0:RP, 1, 0:RK, :].rearrange("p k d -> p (k d)"),
                                 edge_attr[NET * ET:E, :].rearrange("(p k) d -> p (k d)", k=RK)).then_inc(ea_loaded[1], 16)
                    sp.dma_start(rdr[:, :, :], struct[:, S_RD * P:(S_RD + 1) * P].rearrange("(s r) e -> r s e", r=G))\
                        .then_inc(rd_back, 16)
                    sp.wait_ge(t_masked, 1)
                    sp.dma_start(struct[:, S_TI * P:NFIELD * P].rearrange("(s r) f -> r s f", r=G), tg[:, :, :])\
                        .then_inc(t_rows_stored, 16)
                    sp.wait_ge(t_rows_stored, 16)

                @block.tensor
                def _(pe):
                    t = nc.tensor

                    def tile_of(tile, pair, b, full=True):
                        k, p = (KE, P) if full else (RK, RP)
                        done = NGRP * tile
                        pe.wait_ge(ea_loaded[b], 16 * (pair + 1))

                        def product(g, n):
                            pe.wait_ge(turned_kept, done + g + 1)
                            if g >= 2:
                                pe.wait_ge(t_kept, done + g - 1)
                            else:
                                pe.wait_ge(t_kept, done)
                            t.matmul(banks[2 + g % 2][0:L, 0:n * p], vcol[:, :], eat[:, g % 2, 0:n * p],
                                     start=True, stop=True).then_inc(t_made, 1)
                        gs = groups(full)
                        for g, (q, n) in enumerate(gs):
                            pe.wait_ge(turned_kept, done + max(0, g - 1))
                            for s in range(n):
                                last = t.transpose(banks[g % 2][:, s * p:(s + 1) * p], ea[0:p, b, q + s, :], ident[0:p, 0:p])
                            last.then_inc(turned, 1)
                            if g:
                                product(g - 1, gs[g - 1][1])
                        product(len(gs) - 1, gs[-1][1])

                    with pe.Fori(0, NET // 2) as i:
                        tile_of(2 * i, i, 0)
                        tile_of(2 * i + 1, i, 1)
                    tile_of(NET - 1, NET // 2, 0)
                    tile_of(NET, NET // 2, 1, False)

                @block.scalar
                def _(act):
                    def tile_of(tile, full=True):
                        p = P if full else RP
                        done = NGRP * tile
                        for g, (q, n) in enumerate(groups(full)):
                            act.wait_ge(turned, done + g + 1)
                            act.wait_ge(t_made, done + max(0, g - 1))
                            nc.scalar.activation(eat[:, g % 2, 0:n * p], banks[g % 2][:, 0:n * p], ACT.Copy)\
                                .then_inc(turned_kept, 1)
                    with act.Fori(0, NET) as i:
                        tile_of(i)
                    tile_of(NET, False)

                @block.vector
                def _(dve):
                    v = nc.vector

                    def tile_of(tile, pair, b, full=True):
                        k, p = (KE, P) if full else (RK, RP)
                        done = NGRP * tile
                        dve.wait_ge(t_stored[b], 16 * pair)
                        row = trow[:, b, :, :].rearrange("l p k -> l (p k)")[:, 0:p * k].rearrange("l (p k) -> l k p", k=k)
                        for g, (q, n) in enumerate(groups(full)):
                            dve.wait_ge(t_made, done + g + 1)
                            v.tensor_copy(row[:, q:q + n, :], banks[2 + g % 2][0:L, 0:n * p].rearrange("l (k p) -> l k p", p=p))\
                                .then_inc(t_kept, 1)
                    with dve.Fori(0, NET // 2) as i:
                        tile_of(2 * i, i, 0)
                        tile_of(2 * i + 1, i, 1)
                    tile_of(NET - 1, NET // 2, 0)
                    tile_of(NET, NET // 2, 1, False)
                    v.memset(trow[:, 1, :, :].rearrange("l p k -> l (p k)")[:, REST:-(-REST // P) * P], 0.0).then_inc(tail_zeroed, 1)
                    dve.wait_ge(rd_back, 16)
                    v.tensor_scalar(invalid[:, :, :], rdr[:, :, :], 0.0, -BIG, ALU.is_lt, ALU.mult).then_inc(invalid_made, 1)
                    dve.wait_ge(invalid_made, 1)
                    dve.wait_ge(t_gathered, 16 * NSB)
                    for l in range(L):
                        f = tg[:, :, l * P:(l + 1) * P]
                        last = v.tensor_tensor(f, f, invalid[:, :, :], ALU.add)
                    last.then_inc(t_masked, 1)

                @block.gpsimd
                def _(pool):
                    with pool.Fori(0, NET // 2) as i:
                        for b in range(2):
                            pool.wait_ge(t_kept, NGRP * (2 * i + b + 1))
                            pool.dma_start(tv[:, bass.ds((2 * i + b) * KE, KE), :],
                                           trow[:, b, :, :].rearrange("l p k -> l (p k)").rearrange("l (c e) -> l c e", e=P))\
                                .then_inc(t_stored[b], 16)
                    pool.wait_ge(t_kept, NGRP * NET)
                    pool.dma_start(tv[:, (NET - 1) * KE:NET * KE, :],
                                   trow[:, 0, :, :].rearrange("l p k -> l (p k)").rearrange("l (c e) -> l c e", e=P))\
                        .then_inc(t_stored[0], 16)
                    rc = -(-REST // P)
                    pool.wait_ge(t_kept, NGRP * NET + RG)
                    pool.wait_ge(tail_zeroed, 1)
                    pool.dma_start(tv[:, NET * KE:NCH, :],
                                   trow[:, 1, :, :].rearrange("l p k -> l (p k)")[:, 0:rc * P].rearrange("l (c e) -> l c e", e=P))\
                        .then_inc(t_stored[1], 16)
                    pool.wait_ge(t_stored[0], 16 * (NET // 2 + 1))
                    pool.wait_ge(t_stored[1], 16 * (NET // 2 + 1))
                    for s in range(NSB):
                        nc.gpsimd.indirect_dma_start(tg[:, s, :], None, tnat,
                                                     bass.IndirectOffsetOnAxis(cvi[:, s:s + 1], 0)).then_inc(t_gathered, 16)


        with ExitStack() as st:
            sb, ps_, sem = tensors(st)
            nodes = sb("nodes", [P, NT, SLOT])
            hbuf = sb("hbuf", [P, NT, ROW])
            ring = sb("ring", [P, 2 * G, SLOT])
            strow = sb("strow", [G, 2, NFIELD * P])
            ixs = sb("ixs", [P, 2, G], INT32)
            rdb = sb("rdb", [P, 2, P], BF16)
            hot_t = sb("hot_t", [P, 2, 4 * P], BF16)
            hot = sb("hot", [P, 4, P])
            xs = sb("xs", [P, 2, P])
            xt = sb("xt", [P, 2, P])
            dnode = sb("dnode", [P, NT])
            dsplit = sb("dsplit", [P, NT, 3], BF16)
            drest = sb("drest", [P, 2, NT])
            dedge = sb("dedge", [P, G])
            scol = sb("scol", [P, G])
            wcol = sb("wcol", [P, 2, G])
            logit = sb("logit", [G, P])
            logit_u = sb("logit_u", [G, P])
            fmax = sb("fmax", [G, P])
            fmax2 = sb("fmax2", [G, P])
            bmax = sb("bmax", [G, P])
            segmax = sb("segmax", [G, P])
            lastmax = sb("lastmax", [G, P])
            diff = sb("diff", [G, P])
            wrow = sb("wrow", [G, P])
            crow = sb("crow", [1, 2, G + 1])
            brow = sb("brow", [1, 2, G + 1])
            endflags = sb("endflags", [1, G])
            drop = sb("drop", [1, 2])
            fcol = sb("fcol", [P, 1])
            sm = sb("sm", [P, 16, NT])

            names = ["x_loaded", "nodes_ready", "x_staged", "x_turned", "x_turned_kept", "h_made", "h_kept", "h_ready",
                     "table_stored", "struct_used", "slots_free", "index_staged", "rd_rows", "spread", "hot_t_made",
                     "d_picked", "dve_chain3", "logits_cols", "logits_rows", "prefix_max", "tails_row", "carry_row",
                     "carry_cols", "suffix_max", "heads_row", "back_row", "back_cols", "diff_made", "maxima_made",
                     "carry_drop", "w_rows", "carry_factor", "w_cols", "factor_spread", "weights_ready", "weighted",
                     "hot_made", "summed", "acc_done", "fin_chain", "f_made", "f_exp", "h_scaled", "c_made",
                     "centred", "squared", "var_made", "std_made", "out_made", "out_stored", "x_again", "base_set",
                     "pool_paused", "pe_paused", "dve_paused"]
            s = {n: sem("l_" + n) for n in names}
            struct_loaded = [sem("l_struct_loaded0"), sem("l_struct_loaded1")]
            gathered = [sem("l_gathered0"), sem("l_gathered1")]
            NP2 = NSB // 2
            BATCH = [(q, min(4, HG - q)) for q in range(0, HG, 4)]
            NBT = len(BATCH)
            assert NBT % 2 == 0
            num = nodes[:, :, 0:D]
            full, out_rows = N // P, N % P

            def bc_tile(c):
                return c.unsqueeze(2).broadcast_to([P, NT, D])

            with nc.Block() as block:

                @block.sync
                def _(sp):
                    sp.dma_start(num, x.rearrange("(t p) d -> p t d", p=P)).then_inc(s["x_loaded"], 16)
                    with sp.Fori(0, L) as l:
                        sp.wait_ge(s["h_ready"], l + 1)
                        sp.dma_start(table.rearrange("(t p) f -> p t f", p=P), hbuf[:, :, :]).then_inc(s["table_stored"], 16)
                        with sp.Fori(0, NP2) as pr:
                            for h in range(2):
                                g = l * NSB + 2 * pr + h
                                sp.wait_ge(s["struct_used"], g + 1)
                                sp.dma_start(strow[:, h, :], struct[bass.ds((2 * pr + h) * G, G), :])\
                                    .then_inc(struct_loaded[h], 16)
                    sp.wait_ge(s["nodes_ready"], L)
                    sp.dma_start(hbuf[:, :, 0:D], x.rearrange("(t p) d -> p t d", p=P)).then_inc(s["x_again"], 16)
                    sp.wait_ge(s["out_made"], 1)
                    sp.dma_start(out[0:full * P, :].rearrange("(t p) d -> p t d", p=P), num[:, 0:full, :])\
                        .then_inc(s["out_stored"], 16)
                    sp.dma_start(out[full * P:N, :], nodes[0:out_rows, full, 0:D]).then_inc(s["out_stored"], 16)
                    sp.wait_ge(s["out_stored"], 32)

                @block.gpsimd
                def _(pool):
                    p = nc.gpsimd
                    with pool.Fori(0, L) as l:
                        pool.wait_ge(s["table_stored"], 16 * l + 16)
                        pool.sem_inc(s["pool_paused"], 1)
                        with pool.Fori(0, NP2) as pr:
                            for h in range(2):
                                g = l * NSB + 2 * pr + h
                                pool.wait_ge(s["slots_free"], g + 1)
                                pool.sem_inc(s["pool_paused"], 1)
                                p.tensor_copy(ixs[:, h, :], idx[:, bass.ds((2 * pr + h) * G, G)]).then_inc(s["index_staged"], 1)
                                pool.wait_ge(s["index_staged"], g + 1)
                                pool.sem_inc(s["pool_paused"], 1)
                                for k in range(G):
                                    p.indirect_dma_start(ring[:, h * G + k, 0:ROW], None, table,
                                                         bass.IndirectOffsetOnAxis(ixs[:, h, k:k + 1], 0))\
                                        .then_inc(gathered[h], 16)
                        pool.wait_ge(s["c_made"], l + 1)
                        p.tensor_tensor(hbuf[:, :, 0:D], hbuf[:, :, 0:D], bc_tile(sm[:, 12, :]), ALU.mult)\
                            .then_inc(s["h_scaled"], 1)

                @block.tensor
                def _(pe):
                    t = nc.tensor
                    tiles = pe.alloc_registers("tile", HG) if hasattr(pe, "alloc_registers") else \
                        [pe.alloc_register(f"tile{k}") for k in range(HG)]
                    pe.sem_inc(s["struct_used"], 2)
                    pe.sem_inc(s["slots_free"], 2)
                    pe.wait_ge(s["x_loaded"], 16)
                    with pe.Fori(0, L) as l:
                        pe.wait_ge(s["nodes_ready"], l)
                        pe.sem_inc(s["pe_paused"], 1)
                        with pe.Fori(0, NT // 7) as ti:
                            for u in range(7):
                                n = l * NT + 7 * ti + u

                                def product(k):
                                    m = l * NT + 7 * ti + k
                                    pe.wait_ge(s["x_turned_kept"], m + 1)
                                    pe.wait_ge(s["h_kept"], m - 1 if k >= 2 else m - k)
                                    t.matmul(banks[3 + k % 2][:, 0:WXW], xt[:, k % 2, :], wx[:, bass.ds(l, 1), :],
                                             start=True, stop=True).then_inc(s["h_made"], 1)
                                pe.wait_ge(s["x_turned_kept"], n - 1 if u >= 2 else n - u)
                                pe.wait_ge(s["x_staged"], n + 1)
                                t.transpose(banks[u % 2][:, 0:P], xs[:, u % 2, :], ident[:, :])\
                                    .then_inc(s["x_turned"], 1)
                                if u:
                                    product(u - 1)
                            product(6)

                        with pe.Fori(0, NP2) as pr:
                            for h in range(2):
                                g = l * NSB + 2 * pr + h
                                first = (2 * pr + h) * G
                                pe.wait_ge(s["rd_rows"], g + 1)
                                pe.sem_inc(s["pe_paused"], 1)
                                with pe.Fori(0, 2) as q:
                                    t.load(tiles, ntile[0:1, bass.ds(first + q * HG, HG)])

                                    def pick(bi):
                                        b0, n = BATCH[bi]
                                        B = (g * 2 + q) * NBT + bi
                                        pe.wait_ge(s["hot_t_made"], B + 1)
                                        for k in range(n):
                                            tile = pe.snap(tiles[b0 + k], min_val=0, max_val=NT - 1)
                                            last = t.matmul(banks[2][:, bass.ds((q * HG + b0 + k) * 3, 3)],
                                                            hot_t[:, bi % 2, k * P:(k + 1) * P],
                                                            dsplit[:, bass.ds(tile, 1), :], start=True, stop=True)
                                        last.then_inc(s["d_picked"], 1)
                                    for bi, (b0, n) in enumerate(BATCH):
                                        B = (g * 2 + q) * NBT + bi
                                        pe.wait_ge(s["hot_t_made"], B - 1 if bi >= 2 else B - bi)
                                        for k in range(n):
                                            last = t.matmul(banks[bi % 2][:, k * P:(k + 1) * P],
                                                            identb[:, bass.ds(q * HG + b0 + k, 1)].broadcast_to([P, P]),
                                                            rdb[:, h, :], start=True, stop=True)
                                        last.then_inc(s["spread"], 1)
                                        if bi:
                                            pick(bi - 1)
                                    pick(NBT - 1)
                                pe.wait_ge(s["logits_cols"], g + 1)
                                pe.sem_inc(s["pe_paused"], 1)
                                t.transpose(banks[6][0:G, 0:P], scol[:, :], ident[:, :]).then_inc(s["logits_rows"], 1)
                                pe.wait_ge(s["prefix_max"], g + 1)
                                pe.sem_inc(s["pe_paused"], 1)
                                t.transpose(banks[7][0:1, 0:G], fmax[:, P - 1:P], ident[0:G, 0:G]).then_inc(s["tails_row"], 1)
                                pe.wait_ge(s["carry_row"], g + 1)
                                pe.sem_inc(s["pe_paused"], 1)
                                t.transpose(banks[6][0:G, 0:1], crow[:, h, 0:G], ident[0:1, 0:1]).then_inc(s["carry_cols"], 1)
                                pe.wait_ge(s["suffix_max"], g + 1)
                                pe.sem_inc(s["pe_paused"], 1)
                                t.transpose(banks[7][0:1, 0:G], bmax[:, 0:1], ident[0:G, 0:G]).then_inc(s["heads_row"], 1)
                                pe.wait_ge(s["back_row"], g + 1)
                                pe.sem_inc(s["pe_paused"], 1)
                                t.transpose(banks[6][0:G, 0:1], brow[:, h, 1:G + 1], ident[0:1, 0:1]).then_inc(s["back_cols"], 1)
                                pe.wait_ge(s["w_rows"], g + 1)
                                pe.wait_ge(s["maxima_made"], g + 1)
                                pe.sem_inc(s["pe_paused"], 1)
                                t.transpose(banks[7][:, 0:G], wrow[:, :], ident[0:G, 0:G])
                                t.transpose(banks[7][:, G:2 * G], lastmax[:, :], ident[0:G, 0:G])
                                for k in range(L):
                                    last = t.transpose(banks[7][:, (2 + k) * G:(3 + k) * G],
                                                       strow[:, h, (S_TI + k) * P:(S_TI + k + 1) * P], ident[0:G, 0:G])
                                last.then_inc(s["w_cols"], 1)
                                pe.wait_ge(s["w_cols"], g + 1)
                                pe.sem_inc(s["struct_used"], 1)
                                pe.wait_ge(s["carry_factor"], g + 1)
                                t.matmul(banks[6][:, 0:1], ones_row[:, :], drop[:, 1:2], start=True, stop=True)\
                                    .then_inc(s["factor_spread"], 1)
                                with pe.Fori(0, 2) as q:
                                    for u in range(HG):
                                        gv = (g * 2 + q) * HG + u
                                        pe.wait_ge(s["hot_made"], gv + 1)
                                        pe.wait_ge(s["weighted"], gv + 1)
                                        pe.wait_ge(s["acc_done"], gv - 2 if u >= 3 else gv - u)
                                        t.matmul(banks[3 + u % 3][:, 0:SLOT], hot[:, u % 4, :],
                                                 ring[:, bass.ds(h * G + q * HG + u, 1), :], start=True, stop=True)\
                                            .then_inc(s["summed"], 1)
                                pe.wait_ge(s["summed"], (g + 1) * G)
                                pe.sem_inc(s["slots_free"], 1)

                @block.scalar
                def _(act):
                    a = nc.scalar
                    act.wait_ge(s["x_loaded"], 16)
                    with act.Fori(0, L) as l:
                        act.wait_ge(s["nodes_ready"], l)
                        with act.Fori(0, NT // 7) as ti:
                            def stage(k):
                                m = l * NT + 7 * ti + k
                                act.wait_ge(s["x_turned"], m - 1 if k >= 2 else m - k)
                                a.activation(xs[:, k % 2, :], nodes[:, bass.ds(7 * ti + k, 1), 0:D], ACT.Copy)\
                                    .then_inc(s["x_staged"], 1)
                            stage(0)
                            for u in range(7):
                                n = l * NT + 7 * ti + u
                                if u < 6:
                                    stage(u + 1)
                                act.wait_ge(s["x_turned"], n + 1)
                                act.wait_ge(s["h_made"], n - 1 if u >= 2 else n - u)
                                a.activation(xt[:, u % 2, :], banks[u % 2][:, 0:P], ACT.Copy).then_inc(s["x_turned_kept"], 1)
                        with act.Fori(0, NP2) as pr:
                            for h in range(2):
                                g = l * NSB + 2 * pr + h
                                act.wait_ge(s["diff_made"], g + 1)
                                a.activation(wrow[:, :], diff[:, :], ACT.Exp).then_inc(s["w_rows"], 1)
                                act.wait_ge(s["carry_drop"], g + 1)
                                a.activation(drop[:, 1:2], drop[:, 0:1], ACT.Exp).then_inc(s["carry_factor"], 1)
                                act.wait_ge(s["weights_ready"], g + 1)
                                with act.Fori(0, 2) as q:
                                    for u in range(HG):
                                        slot = ring[:, bass.ds(h * G + q * HG + u, 1), 0:D + 1]
                                        a.activation(slot, slot, ACT.Copy, scale=wcol[:, h, bass.ds(q * HG + u, 1)])\
                                            .then_inc(s["weighted"], 1)
                        act.wait_ge(s["f_made"], l + 1)
                        a.activation(sm[:, 8:10, :], sm[:, 6:8, :], ACT.Exp).then_inc(s["f_exp"], 1)
                        act.wait_ge(s["centred"], l + 1)
                        a.activation(hbuf[:, :, 0:D], num, ACT.Square).then_inc(s["squared"], 1)
                        act.wait_ge(s["var_made"], l + 1)
                        a.activation(sm[:, 14, :], sm[:, 13, :], ACT.Sqrt).then_inc(s["std_made"], 1)
                    act.wait_ge(s["centred"], L + 1)
                    a.activation(hbuf[:, :, 0:D], num, ACT.Square).then_inc(s["squared"], 1)
                    act.wait_ge(s["var_made"], L + 1)
                    a.activation(sm[:, 14, :], sm[:, 13, :], ACT.Sqrt).then_inc(s["std_made"], 1)

                @block.vector
                def _(dve):
                    v = nc.vector
                    tiles = [dve.alloc_register(f"vtile{k}") for k in range(HG)]
                    SB_LINKS, LAYER_LINKS, NORM_LINKS = 10, 24, 5
                    PER_LAYER = LAYER_LINKS + NORM_LINKS + NSB * SB_LINKS

                    def normalise(count, link, last):
                        link(v.tensor_reduce(sm[:, 13, :], num, AX.X, ALU.add))
                        link(v.tensor_scalar(sm[:, 13, :], sm[:, 13, :], 1.0 / D, None, ALU.mult))
                        v.tensor_tensor(num, num, bc_tile(sm[:, 13, :]), ALU.subtract).then_inc(s["centred"], 1)
                        dve.wait_ge(s["squared"], count)
                        link(v.tensor_reduce(sm[:, 13, :], hbuf[:, :, 0:D], AX.X, ALU.add))
                        v.tensor_scalar(sm[:, 13, :], sm[:, 13, :], 1.0 / D, LN_EPS, ALU.mult, ALU.add)\
                            .then_inc(s["var_made"], 1)
                        dve.wait_ge(s["std_made"], count)
                        link(v.reciprocal(sm[:, 15, :], sm[:, 14, :]))
                        last(v.tensor_tensor(num, num, bc_tile(sm[:, 15, :]), ALU.mult))

                    dve.wait_ge(s["x_loaded"], 16)
                    v.memset(rdb[:, :, :], 0.0).then_inc(s["base_set"], 1)
                    v.memset(ring[:, :, C_CNT], 1.0).then_inc(s["base_set"], 1)
                    v.memset(brow[:, :, G:G + 1], -BIG).then_inc(s["base_set"], 1)
                    dve.wait_ge(s["base_set"], 3)
                    with dve.Fori(0, L) as l:
                        with dve.Fori(0, NT // 7) as ti:
                            for u in range(7):
                                n = l * NT + 7 * ti + u
                                dve.wait_ge(s["h_made"], n + 1)
                                v.tensor_copy(hbuf[:, bass.ds(7 * ti + u, 1), :], banks[3 + u % 2][:, 0:ROW])
                                v.tensor_copy(dnode[:, bass.ds(7 * ti + u, 1)], banks[3 + u % 2][:, D + 2:D + 3])\
                                    .then_inc(s["h_kept"], 1)
                        dve.wait_ge(s["h_kept"], (l + 1) * NT)
                        v.memset(hbuf[:, :, C_ONE], 1.0).then_inc(s["h_ready"], 1)
                        link = Chain(dve, s["dve_chain3"], l * PER_LAYER)
                        v.memset(crow[:, 1, G:G + 1], -BIG)
                        link(v.tensor_copy(dsplit[:, :, 0], dnode[:, :]))
                        link(v.tensor_tensor(drest[:, 0, :], dnode[:, :], dsplit[:, :, 0], ALU.subtract))
                        link(v.tensor_copy(dsplit[:, :, 1], drest[:, 0, :]))
                        link(v.tensor_tensor(drest[:, 1, :], drest[:, 0, :], dsplit[:, :, 1], ALU.subtract))
                        link(v.tensor_copy(dsplit[:, :, 2], drest[:, 1, :]))
                        link(v.memset(nodes[:, :, :], 0.0))
                        top_links = link.n
                        dve.sem_inc(s["dve_paused"], 1)

                        with dve.Fori(0, NP2) as pr:
                            for h in range(2):
                                g = l * NSB + 2 * pr + h
                                pair = l * NP2 + pr + 1
                                first = (2 * pr + h) * G
                                link = Chain(dve, s["dve_chain3"], l * PER_LAYER + top_links + (2 * pr + h) * SB_LINKS)
                                dve.wait_ge(struct_loaded[h], 16 * pair)
                                field = {f: strow[:, h, f * P:(f + 1) * P] for f in range(NFIELD)}
                                v.tensor_copy(rdb[0:G, h, :], field[S_RD]).then_inc(s["rd_rows"], 1)
                                with dve.Fori(0, 2) as q:
                                    for bi, (b0, n) in enumerate(BATCH):
                                        B = (g * 2 + q) * NBT + bi
                                        dve.wait_ge(s["spread"], B + 1)
                                        dve.wait_ge(s["d_picked"], B - 1 if bi >= 2 else B - bi)
                                        v.tensor_scalar(hot_t[:, bi % 2, 0:n * P], banks[bi % 2][:, 0:n * P],
                                                        iota_col[:, :], None, ALU.is_equal).then_inc(s["hot_t_made"], 1)
                                dve.wait_ge(s["d_picked"], (g + 1) * 2 * NBT)
                                link(v.tensor_reduce(dedge[:, :], banks[2][:, 0:3 * G].rearrange("p (v c) -> p v c", c=3),
                                                     AX.X, ALU.add))
                                link(v.tensor_copy(crow[:, h, 0:1], crow[:, 1 - h, G:G + 1]))
                                link(v.tensor_copy(endflags[:, :], row_flags[:, 1, bass.ds(first, G)]))
                                dve.wait_ge(gathered[h], 16 * G * pair)
                                v.tensor_tensor(scol[:, :], ring[:, h * G:(h + 1) * G, C_S], dedge[:, :], ALU.add)\
                                    .then_inc(s["logits_cols"], 1)
                                dve.wait_ge(s["logits_rows"], g + 1)
                                link(v.tensor_tensor(logit_u[:, :], banks[6][0:G, 0:P],
                                                     strow[:, h, bass.ds(S_TI * P + l * P, P)], ALU.add))
                                link(v.scalar_tensor_tensor(logit[:, :], logit_u[:, :], SLOPE, logit_u[:, :],
                                                            ALU.mult, ALU.max))
                                v.tensor_tensor_scan(fmax[:, :], field[S_RF], logit[:, :], -BIG, ALU.add, ALU.max)\
                                    .then_inc(s["prefix_max"], 1)
                                dve.wait_ge(s["tails_row"], g + 1)
                                v.tensor_tensor_scan(crow[:, h, 1:G + 1], row_flags[:, 0, bass.ds(first, G)],
                                                     banks[7][0:1, 0:G], crow[:, h, 0:1], ALU.add, ALU.max)\
                                    .then_inc(s["carry_row"], 1)
                                dve.wait_ge(s["carry_cols"], g + 1)
                                link(v.scalar_tensor_tensor(fmax2[:, :], field[S_OF], banks[6][0:G, 0:1], fmax[:, :],
                                                            ALU.add, ALU.max))
                                v.tensor_tensor_scan(bmax[:, ::-1], field[S_RB][:, ::-1], fmax2[:, ::-1], -BIG,
                                                     ALU.add, ALU.max).then_inc(s["suffix_max"], 1)
                                dve.wait_ge(s["heads_row"], g + 1)
                                v.tensor_tensor_scan(brow[:, h, 0:G][:, ::-1], endflags[:, ::-1],
                                                     banks[7][0:1, 0:G][:, ::-1], -BIG, ALU.add, ALU.max)\
                                    .then_inc(s["back_row"], 1)
                                dve.wait_ge(s["back_cols"], g + 1)
                                link(v.scalar_tensor_tensor(segmax[:, :], field[S_OB], banks[6][0:G, 0:1], bmax[:, :],
                                                            ALU.add, ALU.max))
                                v.tensor_tensor(diff[:, :], logit[:, :], segmax[:, :], ALU.subtract).then_inc(s["diff_made"], 1)
                                v.scalar_tensor_tensor(lastmax[:, :], field[S_RB], -1.0 / BIG, segmax[:, :],
                                                       ALU.mult, ALU.mult).then_inc(s["maxima_made"], 1)
                                link(v.tensor_tensor(drop[:, 0:1], crow[:, h, 0:1], brow[:, h, 0:1], ALU.subtract))
                                v.tensor_scalar(drop[:, 0:1], drop[:, 0:1], 0.0, None, ALU.min).then_inc(s["carry_drop"], 1)
                                dve.wait_ge(s["w_cols"], g + 1)
                                v.tensor_copy(wcol[:, h, :], banks[7][:, 0:G])
                                v.tensor_copy(ring[:, h * G:(h + 1) * G, C_M:C_T + L].rearrange("p v c -> p c v"),
                                              banks[7][:, G:(2 + L) * G].rearrange("p (c v) -> p c v", c=1 + L))\
                                    .then_inc(s["weights_ready"], 1)
                                dve.wait_ge(s["factor_spread"], g + 1)
                                link(v.scalar_tensor_tensor(fcol[:, :], carry_hot[:, bass.ds(2 * pr + h, 1)],
                                                            banks[6][:, 0:1], carry_not[:, bass.ds(2 * pr + h, 1)],
                                                            ALU.mult, ALU.add))
                                v.load(tiles[0:1], ntile[0:1, bass.ds(first, 1)])
                                tile = dve.snap(tiles[0], min_val=0, max_val=NT - 1)
                                dve.wait_ge(s["acc_done"], g * G)
                                own = nodes[:, bass.ds(tile, 1), 0:D + 1]
                                link(v.tensor_scalar(own, own, fcol[:, :], None, ALU.mult))
                                assert link.n == SB_LINKS, link.n
                                dve.sem_inc(s["dve_paused"], 1)

                                with dve.Fori(0, 2) as q:
                                    v.load(tiles, ntile[0:1, bass.ds(first + q * HG, HG)])

                                    def accumulate(u):
                                        gv = (g * 2 + q) * HG + u
                                        dve.wait_ge(s["summed"], gv + 1)
                                        dve.wait_ge(s["acc_done"], gv)
                                        tile = dve.snap(tiles[u], min_val=0, max_val=NT - 1)
                                        own = nodes[:, bass.ds(tile, 1), :]
                                        v.tensor_tensor(own, own, banks[3 + u % 3][:, 0:SLOT], ALU.add)\
                                            .then_inc(s["acc_done"], 1)
                                    for u in range(HG):
                                        v.tensor_scalar(hot[:, u % 4, :], iota_row[:, :],
                                                        rdcol[:, bass.ds(first + q * HG + u, 1)], None, ALU.is_equal)\
                                            .then_inc(s["hot_made"], 1)
                                        if u >= 2:
                                            accumulate(u - 2)
                                    accumulate(HG - 2)
                                    accumulate(HG - 1)

                        link = Chain(dve, s["dve_chain3"], l * PER_LAYER + top_links + NSB * SB_LINKS)
                        dve.wait_ge(s["acc_done"], (l + 1) * NV)
                        cnt = nodes[:, :, C_CNT]
                        link(v.tensor_scalar(sm[:, 0, :], cnt, 1.0, None, ALU.max))
                        link(v.reciprocal(sm[:, 1, :], sm[:, 0, :]))
                        link(v.tensor_tensor(sm[:, 2, :], nodes[:, :, bass.ds(C_T + l, 1)].rearrange("p t o -> p (t o)"),
                                             sm[:, 1, :], ALU.mult))
                        link(v.tensor_tensor(sm[:, 2, :], sm[:, 2, :], hbuf[:, :, C_S], ALU.add))
                        link(v.tensor_tensor(sm[:, 2, :], sm[:, 2, :], dnode[:, :], ALU.add))
                        link(v.scalar_tensor_tensor(sm[:, 3, :], sm[:, 2, :], SLOPE, sm[:, 2, :], ALU.mult, ALU.max))
                        link(v.tensor_scalar(sm[:, 4, :], cnt, 0.0, -BIG, ALU.is_equal, ALU.mult))
                        link(v.tensor_tensor(sm[:, 4, :], sm[:, 4, :], nodes[:, :, C_M], ALU.add))
                        link(v.tensor_tensor(sm[:, 5, :], sm[:, 4, :], sm[:, 3, :], ALU.max))
                        link(v.tensor_tensor(sm[:, 6, :], sm[:, 4, :], sm[:, 5, :], ALU.subtract))
                        v.tensor_tensor(sm[:, 7, :], sm[:, 3, :], sm[:, 5, :], ALU.subtract).then_inc(s["f_made"], 1)
                        dve.wait_ge(s["f_exp"], l + 1)
                        link(v.tensor_tensor(sm[:, 10, :], nodes[:, :, C_ONE], sm[:, 8, :], ALU.mult))
                        link(v.tensor_tensor(sm[:, 10, :], sm[:, 10, :], sm[:, 9, :], ALU.add))
                        link(v.reciprocal(sm[:, 11, :], sm[:, 10, :]))
                        v.tensor_tensor(sm[:, 12, :], sm[:, 9, :], sm[:, 11, :], ALU.mult).then_inc(s["c_made"], 1)
                        link(v.tensor_tensor(sm[:, 11, :], sm[:, 8, :], sm[:, 11, :], ALU.mult))
                        link(v.tensor_tensor(num, num, bc_tile(sm[:, 11, :]), ALU.mult))
                        dve.wait_ge(s["h_scaled"], l + 1)
                        link(v.tensor_tensor(num, num, hbuf[:, :, 0:D], ALU.add))

                        def param(c):
                            return par[:, bass.ds(l, 1), c, :].broadcast_to([P, NT, D])
                        link(v.tensor_tensor(num, num, param(0), ALU.add))
                        normalise(l + 1, link, link)
                        link(v.tensor_tensor(num, num, param(1), ALU.mult))
                        assert top_links + link.n == PER_LAYER - NSB * SB_LINKS, top_links + link.n
                        v.tensor_tensor(num, num, param(2), ALU.add).then_inc(s["nodes_ready"], 1)
                    link = Chain(dve, s["dve_chain3"], L * PER_LAYER)
                    dve.wait_ge(s["x_again"], 16)
                    dve.wait_ge(s["nodes_ready"], L)
                    link(v.tensor_tensor(num, num, hbuf[:, :, 0:D], ALU.add))
                    normalise(L + 1, link, lambda ins: ins.then_inc(s["out_made"], 1))


def kernel(x, src, dst, edge_attr_128, L0_gnn_W, L0_gnn_att_src, L0_gnn_att_dst, L0_gnn_W_e,
           L0_gnn_att_edge, L0_gnn_bias, L0_gnn_ln_gamma, L0_gnn_ln_beta):
    import concourse.bacc as bacc
    from concourse.bass_utils import run_bass_kernel_spmd as run

    xp = np.zeros((NT * P, D), np.float32)
    xp[:N] = np.asarray(x)
    d = np.full(NCH * P + 2, 1 << 20, np.int32)
    d[0] = -1
    d[1:E + 1] = np.asarray(dst)
    s = np.zeros(NCH * P, np.int32)
    s[:E] = np.asarray(src)
    ei = np.empty((NCH, EIW), np.int32)
    for k in range(P + 2):
        ei[:, k] = d[k:k + (NCH - 1) * P + 1:P]
    ei[:, P + 2:] = s.reshape(NCH, P)
    last = np.full(NCH, N - 1, np.int32)
    last[:NCH - 1] = np.asarray(dst)[P - 1::P][:NCH - 1]
    att = np.empty((D, 3 * L), np.float32)
    for l in range(L):
        att[:, 3 * l] = np.asarray(L0_gnn_att_src)[l]
        att[:, 3 * l + 1] = np.asarray(L0_gnn_att_dst)[l]
        att[:, 3 * l + 2] = np.asarray(L0_gnn_att_edge)[l]
    par = np.stack([np.asarray(L0_gnn_bias), np.asarray(L0_gnn_ln_gamma), np.asarray(L0_gnn_ln_beta)], 1).reshape(-1)
    w = np.asarray(L0_gnn_W)
    arrays = {
        "x": xp, "ei": ei, "chunk_last": last, "edge_attr": np.ascontiguousarray(edge_attr_128),
        "w": np.ascontiguousarray(w), "wt": np.ascontiguousarray(w.transpose(0, 2, 1)),
        "wet": np.ascontiguousarray(np.asarray(L0_gnn_W_e).transpose(0, 2, 1)), "att": att, "params": par,
    }
    nc = bacc.Bacc("TRN2", target_bir_lowering=False, num_devices=1)
    args = [nc.dram_tensor(f"in_{n}", a.shape, mybir.dt.from_np(a.dtype), kind="ExternalInput").ap()
            for n, a in arrays.items()]
    args.append(nc.dram_tensor("out_0", (N, D), FP32, kind="ExternalOutput").ap())
    build(nc, *args)
    r = run(nc, [{f"in_{n}": a for n, a in arrays.items()}], core_ids=[0])
    return r.results[0]["out_0"]
```

```python
import numpy as np
import concourse.bass as bass
from concourse import mybir
from contextlib import ExitStack

FP32 = mybir.dt.float32
INT32 = mybir.dt.int32
BF16 = mybir.dt.bfloat16
ALU = mybir.AluOpType
ACT = mybir.ActivationFunctionType
AX = mybir.AxisListType

P = 128
N, E, D, L = 6250, 200000, 128, 3
NT = -(-N // P)
NCH = -(-E // P)
NVIS = NCH + NT - 1
NSB = -(-NVIS // 64)
NSB += NSB % 2
G = -(-NVIS // NSB)
G += G % 2
HG = G // 2
NV = NSB * G
BIG = 2.0 ** 100
LN_EPS = 1e-5
SLOPE = 0.2

C_ONE, C_S, C_M, C_T, C_CNT = D, D + 1, D + 1, D + 2, D + 2 + L
ROW = D + 2
SLOT = C_CNT + 1
S_RF, S_RB, S_OF, S_OB, S_RD = range(5)
NFIELD = 5
EIW = P + 2 + P

KE = 8
ET = P * KE
NET = E // ET
REST = E - NET * ET
RK = next(k for k in range(1, KE + 1) if REST % k == 0 and REST // k <= P and (REST // k) % 16 == 0)
RP = REST // RK
SUB = 4
NGRP = KE // SUB
assert 0 < RK <= SUB and NGRP == 2
EPS_ = -(-G * P // ET)
EPAIRS = (NET - 2 * EPS_) // (2 * EPS_)
ALONG = EPAIRS * 2 * EPS_
AHEAD = 2 * EPS_
EXTRA = NET - ALONG - AHEAD
WXW = D + 3


class Chain:

    def __init__(self, eng, sem, base=0):
        self.eng, self.sem, self.base, self.n = eng, sem, base, 0

    def __call__(self, ins):
        self.n += 1
        ins.then_inc(self.sem, 1)
        self.eng.wait_ge(self.sem, self.base + self.n)


def build(nc, x, ei, chunk_last, edge_attr, w, wt, wet, att, params, out):
    table = nc.dram_tensor("table", (NT * P, ROW), FP32).ap()
    tnat = nc.dram_tensor("tnat", (NCH, L * P), FP32).ap()
    struct = nc.dram_tensor("struct", (NV, NFIELD * P), FP32).ap()
    tirows = nc.dram_tensor("tirows", (NV, L * P), FP32).ap()
    perv = nc.dram_tensor("perv", (2, NV), FP32).ap()
    perv_i = nc.dram_tensor("perv_i", (1, NV), INT32).ap()

    ctx = ExitStack()

    def tensors(stack):
        def sb(name, shape, dt=FP32):
            return stack.enter_context(nc.sbuf_tensor(name, shape, dt))

        def ps(name):
            return stack.enter_context(nc.psum_tensor(name, [P, 512], FP32))

        def sem(name):
            return stack.enter_context(nc.semaphore(name))
        return sb, ps, sem

    with ctx:
        sb, ps_, sem = tensors(ctx)
        banks = [ps_(f"bank{i}") for i in range(8)]
        ident = sb("ident", [P, P])
        identb = sb("identb", [P, P], BF16)
        iota_row = sb("iota_row", [P, P])
        iota_col = sb("iota_col", [P, 1])
        ones_row = sb("ones_row", [1, P])
        idx = sb("idx", [P, NV], INT32)
        rdcol = sb("rdcol", [P, NV])
        carry_hot = sb("carry_hot", [P, NSB])
        carry_not = sb("carry_not", [P, NSB])
        ntile = sb("ntile", [1, NV + G], INT32)
        wx = sb("wx", [P, L, WXW])
        vcol = sb("vcol", [P, L])
        cvi = sb("cvi", [G, NSB], INT32)
        par = sb("par", [P, L, 3, P])

        with ExitStack() as st:
            sb, ps_, sem = tensors(st)
            cl = sb("cl", [P, NCH], INT32)
            clf = sb("clf", [P, NCH])
            vid = sb("vid", [G, NSB])
            ncol = sb("ncol", [P, 1])
            ndiag = sb("ndiag", [P, NT + 1])
            nrow = sb("nrow", [G, NT + 1])
            cmp = sb("cmp", [G, NSB, NT])
            nv = sb("nv", [G, NSB])
            n128 = sb("n128", [G, NSB])
            cvf = sb("cvf", [G, NSB])
            HS = NSB // 2
            eit = sb("eit", [G, HS, EIW], INT32)
            names = ["rd", "valid", "rf", "rb", "of", "ob", "tmp", "srcf"]
            a = {n: sb(f"a_{n}", [G, HS, P]) for n in names}
            r1 = sb("r1", [1, HS, P])
            r2 = sb("r2", [1, HS, P])
            cb = sb("cb", [1, NSB])
            pv = sb("pv", [NSB, 3, G])
            pvi = sb("pvi", [NSB, G], INT32)
            rowv = sb("rowv", [G, 3, NSB])
            clc = sb("clc", [P, NCH])
            attc = sb("attc", [P, 3 * L])
            wts = sb("wts", [P, 2, L, P])
            ones_g = sb("ones_g", [P, G])
            zeros = sb("zeros", [P, L * P])
            t_cleared = sem("t_cleared")
            dst_loaded = sem("dst_loaded")
            weights_loaded = sem("weights_loaded")
            consts_made = sem("consts_made")
            ones_made = sem("ones_made")
            dve_chain = sem("dve_chain")
            tile_starts = sem("tile_starts")
            starts_spread = sem("starts_spread")
            chunks_known = sem("chunks_known")
            ints_gathered = sem("ints_gathered")
            masks_made = sem("masks_made")
            masks_stored = sem("masks_stored")
            columns_turned = sem("columns_turned")
            columns_kept = sem("columns_kept")
            half_used = sem("half_used")
            carry_found = sem("carry_found")
            carry_spread = sem("carry_spread")
            row_turned = sem("row_turned")
            row_made = sem("row_made")
            row_stored = sem("row_stored")
            row_back = sem("row_back")
            att_applied = sem("att_applied")
            with nc.Block() as block:
                NB = -(-HS // 8)

                @block.scalar
                def _(act):
                    act.wait_ge(consts_made, 8)
                    whole = NCH // P * P
                    act.dma_start(tnat[0:whole, :].rearrange("(c p) f -> p c f", p=P),
                                  zeros[:, :].unsqueeze(1).broadcast_to([P, NCH // P, L * P])).then_inc(t_cleared, 16)
                    act.dma_start(tnat[whole:NCH, :], zeros[0:NCH - whole, :]).then_inc(t_cleared, 16)
                    act.wait_ge(t_cleared, 32)

                @block.sync
                def _(sp):
                    sp.dma_start(cl[:, :], chunk_last.partition_broadcast(P)).then_inc(dst_loaded, 16)
                    sp.dma_start(attc[:, :], att).then_inc(weights_loaded, 16)
                    for l in range(L):
                        sp.dma_start(wx[:, l, 0:D], w[l]).then_inc(weights_loaded, 16)
                        sp.dma_start(wts[:, 0, l, :], wt[l]).then_inc(weights_loaded, 16)
                        sp.dma_start(wts[:, 1, l, :], wet[l]).then_inc(weights_loaded, 16)
                    sp.dma_start(par[:, :, :, :].rearrange("p l c d -> p (l c d)"),
                                 params.partition_broadcast(P)).then_inc(weights_loaded, 16)
                    for hh in range(2):
                        rows = struct[hh * HS * G:(hh + 1) * HS * G, :].rearrange("(s r) f -> r s f", r=G)
                        sp.wait_ge(masks_made, hh + 1)
                        for f, n in enumerate(["rf", "rb", "of", "ob", "rd"]):
                            sp.dma_start(rows[:, :, f * P:(f + 1) * P], a[n][:, :, :]).then_inc(masks_stored, 16)
                    sp.wait_ge(row_made, 1)
                    for f in range(2):
                        sp.dma_start(perv[f, :].rearrange("(s r) -> s r", r=G), pv[:, f + 1, :]).then_inc(row_stored, 16)
                    sp.dma_start(perv_i[0, :].rearrange("(s r) -> s r", r=G), pvi[:, :]).then_inc(row_stored, 16)
                    sp.wait_ge(row_stored, 48)
                    sp.dma_start(ntile[:, 0:NV], perv_i).then_inc(row_back, 16)
                    sp.wait_ge(row_back, 16)
                    sp.wait_ge(masks_stored, 16 * 10)

                @block.gpsimd
                def _(pool):
                    nc.gpsimd.iota(iota_row[:, :], [[1, P]], base=0, channel_multiplier=0,
                                   allow_small_or_imprecise_dtypes=True).then_inc(consts_made, 1)
                    nc.gpsimd.iota(iota_col[:, :], [[1, 1]], base=0, channel_multiplier=1,
                                   allow_small_or_imprecise_dtypes=True).then_inc(consts_made, 1)
                    nc.gpsimd.iota(vid[:, :], [[G, NSB]], base=0, channel_multiplier=1,
                                   allow_small_or_imprecise_dtypes=True).then_inc(consts_made, 1)
                    nc.gpsimd.memset(ones_row[:, :], 1.0).then_inc(consts_made, 1)
                    nc.gpsimd.memset(ones_g[:, :], 1.0).then_inc(consts_made, 1)
                    nc.gpsimd.memset(ident[:, :], 0.0).then_inc(consts_made, 1)
                    pool.wait_ge(consts_made, 6)
                    nc.gpsimd.affine_select(out=ident[:, :], in_=ident[:, :], compare_op=ALU.not_equal, fill=1.0,
                                            base=0, pattern=[[-1, P]], channel_multiplier=1).then_inc(consts_made, 1)
                    nc.gpsimd.memset(ntile[:, NV:NV + G], 0)
                    nc.gpsimd.memset(zeros[:, :], 0.0).then_inc(consts_made, 1)
                    pool.wait_ge(chunks_known, 1)
                    for hh in range(2):
                        if hh:
                            pool.wait_ge(half_used, 1)
                        for s in range(HS):
                            c = hh * HS + s
                            nc.gpsimd.indirect_dma_start(
                                eit[:, s, :], None, ei,
                                bass.IndirectOffsetOnAxis(cvi[:, c:c + 1], 0)).then_inc(ints_gathered, 16)

                @block.vector
                def _(dve):
                    v = nc.vector
                    link = Chain(dve, dve_chain)
                    dve.wait_ge(consts_made, 7)
                    link(v.tensor_copy(identb[:, :], ident[:, :]))
                    dve.wait_ge(dst_loaded, 16)
                    link(v.tensor_single_scalar(cl[:, :], cl[:, :], 7, ALU.arith_shift_right))
                    link(v.tensor_copy(clf[:, :], cl[:, :]))
                    link(v.tensor_scalar(clc[:, :], clf[:, :], iota_col[:, :], None, ALU.is_lt))
                    link(v.tensor_reduce(ncol[:, :], clc[:, :], AX.X, ALU.add))
                    link(v.tensor_scalar(ncol[:, :], ncol[:, :], float(NCH - 1), iota_col[:, :], ALU.min, ALU.add))
                    v.tensor_scalar(ndiag[:, :], ident[:, 0:NT + 1], ncol[:, :], None, ALU.mult).then_inc(tile_starts, 1)
                    dve.wait_ge(starts_spread, 1)
                    link(v.tensor_copy(nrow[:, :], banks[0][0:G, 0:NT + 1]))
                    link(v.tensor_tensor(cmp[:, :, :], vid[:, :].unsqueeze(2).broadcast_to([G, NSB, NT]),
                                         nrow[:, 1:NT + 1].unsqueeze(1).broadcast_to([G, NSB, NT]), ALU.is_ge))
                    link(v.tensor_reduce(nv[:, :], cmp[:, :, :], AX.X, ALU.add))
                    link(v.tensor_scalar(n128[:, :], nv[:, :], float(P), None, ALU.mult))
                    link(v.tensor_tensor(cvf[:, :], vid[:, :], nv[:, :], ALU.subtract))
                    link(v.tensor_scalar(rowv[:, 0, :], nv[:, :], float(NT - 1), None, ALU.min))
                    v.tensor_copy(cvi[:, :], cvf[:, :]).then_inc(chunks_known, 1)
                    for hh in range(2):
                        cols = slice(hh * HS, (hh + 1) * HS)
                        dve.wait_ge(ints_gathered, 16 * HS * (hh + 1))
                        if hh:
                            dve.wait_ge(masks_stored, 80)
                            dve.wait_ge(columns_turned, NB)
                        dst = eit[:, :, 1:P + 1]
                        link(v.tensor_tensor(a["rd"][:, :, :], dst,
                                             n128[:, cols].unsqueeze(2).broadcast_to([G, HS, P]), ALU.subtract))
                        link(v.tensor_scalar(a["tmp"][:, :, :], a["rd"][:, :, :], 0.0, None, ALU.is_ge))
                        link(v.scalar_tensor_tensor(a["valid"][:, :, :], a["rd"][:, :, :], float(P), a["tmp"][:, :, :],
                                                    ALU.is_lt, ALU.mult))
                        link(v.scalar_tensor_tensor(a["tmp"][:, :, :], a["rd"][:, :, :], 1.0, a["valid"][:, :, :],
                                                    ALU.add, ALU.mult))
                        link(v.tensor_scalar(a["rd"][:, :, :], a["tmp"][:, :, :], -1.0, None, ALU.add))
                        for n, off in (("rf", 0), ("rb", 2)):
                            link(v.tensor_tensor(a["tmp"][:, :, :], dst, eit[:, :, off:off + P], ALU.not_equal))
                            link(v.scalar_tensor_tensor(a[n][:, :, :], a["tmp"][:, :, :], -BIG, a["valid"][:, :, :],
                                                        ALU.mult, ALU.mult))
                        link(v.tensor_copy(a["srcf"][:, :, :], eit[:, :, P + 2:EIW]))
                        for s in range(HS):
                            v.tensor_tensor_scan(a["of"][:, s, :], a["rf"][:, s, :], a["rf"][:, s, :], 0.0,
                                                 ALU.min, ALU.min)
                            last = v.tensor_tensor_scan(a["ob"][:, s, ::-1], a["rb"][:, s, ::-1], a["rb"][:, s, ::-1],
                                                        0.0, ALU.min, ALU.min)
                        last.then_inc(masks_made, 1)
                        dve.wait_ge(masks_made, hh + 1)
                        link(v.tensor_copy(rowv[:, 1, cols], a["of"][:, :, P - 1]))
                        v.tensor_copy(rowv[:, 2, cols], a["ob"][:, :, 0]).then_inc(half_used, 1)
                        dve.wait_ge(half_used, hh + 1)
                        va = a["valid"][0:1, :, :]
                        link(v.tensor_tensor(r1[:, :, 1:P], va[:, :, 1:P], va[:, :, 0:P - 1], ALU.is_gt))
                        link(v.tensor_copy(r1[:, :, 0:1], va[:, :, 0:1]))
                        link(v.tensor_scalar(r2[:, :, :], a["rf"][0:1, :, :], 0.0, None, ALU.is_equal))
                        link(v.tensor_tensor(r1[:, :, :], r1[:, :, :], r2[:, :, :], ALU.mult))
                        link(v.scalar_tensor_tensor(r2[:, :, :], a["rd"][0:1, :, :], 1.0, r1[:, :, :], ALU.add, ALU.mult))
                        link(v.tensor_reduce(cb[:, cols], r2[:, :, :], AX.X, ALU.add))
                        for b in range(NB):
                            c0 = (hh * HS + b * 8) * G
                            c1 = (hh * HS + min(HS, b * 8 + 8)) * G
                            dve.wait_ge(columns_turned, hh * NB + b + 1)
                            v.tensor_copy(idx[:, c0:c1], banks[2 * b][:, 0:c1 - c0])
                            v.tensor_copy(rdcol[:, c0:c1], banks[2 * b + 1][:, 0:c1 - c0]).then_inc(columns_kept, 1)
                    v.tensor_scalar(cb[:, :], cb[:, :], -1.0, None, ALU.add).then_inc(carry_found, 1)
                    dve.wait_ge(carry_spread, 1)
                    v.tensor_scalar(carry_hot[:, :], banks[4][:, 0:NSB], iota_col[:, :], None, ALU.is_equal)
                    v.tensor_scalar(carry_not[:, :], banks[4][:, 0:NSB], iota_col[:, :], None, ALU.not_equal)
                    dve.wait_ge(row_turned, 1)
                    link(v.tensor_copy(pv[:, :, :], banks[5][0:NSB, 0:3 * G].rearrange("p (f g) -> p f g", f=3)))
                    v.tensor_copy(pvi[:, :], pv[:, 0, :]).then_inc(row_made, 1)
                    dve.wait_ge(weights_loaded, 16 * (3 * L + 2))
                    dve.wait_ge(att_applied, 1)
                    v.tensor_copy(wx[:, :, D + 1:D + 3], banks[6][:, 0:2 * L].rearrange("p (l c) -> p l c", c=2))
                    v.tensor_copy(vcol[:, :], banks[6][:, 2 * L:3 * L])
                    v.memset(wx[:, :, D:D + 1], 0.0)

                @block.tensor
                def _(pe):
                    t = nc.tensor
                    pe.wait_ge(tile_starts, 1)
                    t.matmul(banks[0][0:G, 0:NT + 1], ones_g[:, :], ndiag[:, :], start=True, stop=True)\
                        .then_inc(starts_spread, 1)
                    for hh in range(2):
                        pe.wait_ge(masks_made, hh + 1)
                        for b in range(NB):
                            if hh:
                                pe.wait_ge(columns_kept, b + 1)
                            for s in range(b * 8, min(HS, b * 8 + 8)):
                                o = (s - b * 8) * G
                                t.transpose(banks[2 * b][:, o:o + G], a["srcf"][:, s, :], ident[0:G, 0:G])
                                last = t.transpose(banks[2 * b + 1][:, o:o + G], a["rd"][:, s, :], ident[0:G, 0:G])
                            last.then_inc(columns_turned, 1)
                    pe.wait_ge(carry_found, 1)
                    t.matmul(banks[4][:, 0:NSB], ones_row[:, :], cb[:, :], start=True, stop=True).then_inc(carry_spread, 1)
                    for f in range(3):
                        last = t.transpose(banks[5][0:NSB, f * G:(f + 1) * G], rowv[:, f, :], ident[0:G, 0:G])
                    last.then_inc(row_turned, 1)
                    pe.wait_ge(weights_loaded, 16 * (3 * L + 2))
                    for l in range(L):
                        for j in range(3):
                            col = 2 * l + j if j < 2 else 2 * L + l
                            last = t.matmul(banks[6][:, col:col + 1], wts[:, j // 2, l, :],
                                            attc[:, 3 * l + j:3 * l + j + 1], start=True, stop=True)
                    last.then_inc(att_applied, 1)


        with ExitStack() as st:
            sb, ps_, sem = tensors(st)
            nodes = sb("nodes", [P, NT, SLOT])
            hbuf = sb("hbuf", [P, NT, ROW])
            ring = sb("ring", [P, 2 * G, SLOT])
            strow = sb("strow", [G, 2, NFIELD * P])
            tirow = sb("tirow", [G, 2, L * P])
            flags = sb("flags", [1, 2, 2, G])
            ixs = sb("ixs", [P, 2, G], INT32)
            cvs = sb("cvs", [G, 2], INT32)
            rdb = sb("rdb", [P, 2, P], BF16)
            hot_t = sb("hot_t", [P, 2, 4 * P], BF16)
            hot = sb("hot", [P, 4, P])
            xs = sb("xs", [P, 2, P])
            xt = sb("xt", [P, 2, P])
            dnode = sb("dnode", [P, NT])
            dsplit = sb("dsplit", [P, NT, 3], BF16)
            drest = sb("drest", [P, 2, NT])
            dedge = sb("dedge", [P, 2, G])
            scol = sb("scol", [P, G])
            wcol = sb("wcol", [P, 2, G])
            logit = sb("logit", [G, P])
            logit_u = sb("logit_u", [G, P])
            fmax = sb("fmax", [G, P])
            fmax2 = sb("fmax2", [G, P])
            bmax = sb("bmax", [G, P])
            segmax = sb("segmax", [G, P])
            lastmax = sb("lastmax", [G, P])
            diff = sb("diff", [G, P])
            wrow = sb("wrow", [G, P])
            outside = sb("outside", [G, P])
            crow = sb("crow", [1, 2, G + 1])
            brow = sb("brow", [1, 2, G + 1])
            drop = sb("drop", [1, 2])
            fcol = sb("fcol", [P, 1])
            sm = sb("sm", [P, 16, NT])
            ea = sb("ea", [P, 2, KE, D])
            eat = sb("eat", [P, 2, SUB * P])
            trow = sb("trow", [L, 2, P, KE])

            names = ["x_loaded", "nodes_ready", "x_staged", "x_turned", "x_turned_kept", "h_made", "h_kept", "h_ready",
                     "table_stored", "struct_used", "slots_free", "index_staged", "rd_rows", "spread", "hot_t_made",
                     "d_picked", "dve_links", "logits_cols", "logits_rows", "prefix_max", "tails_row", "carry_row",
                     "carry_cols", "suffix_max", "heads_row", "back_row", "back_cols", "diff_made", "maxima_made",
                     "carry_drop", "w_rows", "carry_factor", "w_cols", "factor_spread", "weights_ready", "weighted",
                     "hot_made", "summed", "acc_done", "f_made", "f_exp", "h_scaled", "c_made",
                     "centred", "squared", "var_made", "std_made", "out_made", "out_stored", "x_again", "base_set",
                     "ea_turned", "ea_kept", "t_made", "t_kept", "t_masked",
                     "chunk_staged", "d_taken", "fcol_made", "outside_made", "act_paused",
                     "pool_paused", "pe_paused", "dve_paused"]
            s = {n: sem("l_" + n) for n in names}
            struct_loaded = [sem("l_struct_loaded0"), sem("l_struct_loaded1")]
            ti_loaded = [sem("l_ti_loaded0"), sem("l_ti_loaded1")]
            ti_stored = [sem("l_ti_stored0"), sem("l_ti_stored1")]
            t_gathered = [sem("l_t_gathered0"), sem("l_t_gathered1")]
            gathered = [sem("l_gathered0"), sem("l_gathered1")]
            ea_loaded = [sem("l_ea_loaded0"), sem("l_ea_loaded1")]
            t_stored = [sem("l_t_stored0"), sem("l_t_stored1")]
            NP2 = NSB // 2
            BATCH = [(q, min(4, HG - q)) for q in range(0, HG, 4)]
            NBT = len(BATCH)
            DSB = 2 * NBT
            DLAYER = (NSB + 1) * DSB
            assert NBT % 2 == 0 and NBT == EPS_ * NGRP // 2
            num = nodes[:, :, 0:D]
            full, out_rows = N // P, N % P
            tv = tnat.rearrange("c (l e) -> l c e", l=L)

            def bc_tile(c):
                return c.unsqueeze(2).broadcast_to([P, NT, D])

            def item_of_tile(i):
                return i + EXTRA + 1
            PRE = [(0, None)] + [(1 + k, NET - EXTRA + k) for k in range(EXTRA)] + \
                  [(item_of_tile(i), i) for i in range(AHEAD)]
            LAST_ITEM = item_of_tile(AHEAD + ALONG - 1)
            PI = item_of_tile(0) % 2

            J0 = item_of_tile(AHEAD)
            assert EXTRA >= 2 and (EPS_ // 2) % 2 == 0

            def ea_source(j, tile):
                if tile is None:
                    return (ea[0:RP, 0, 0:RK, :].rearrange("p k d -> p (k d)"),
                            edge_attr[NET * ET:E, :].rearrange("(p k) d -> p (k d)", k=RK))
                return (ea[:, j, :, :].rearrange("p k d -> p (k d)"),
                        edge_attr[bass.ds(tile * ET, ET), :].rearrange("(p k) d -> p (k d)", k=KE))

            NITEMS = LAST_ITEM + 1
            T_STORES = [(NITEMS + 1) // 2, NITEMS // 2]

            with nc.Block() as block:

                @block.sync
                def _(sp):
                    def load_ea(j, par, tile):
                        dst, src = ea_source(par, tile)
                        sp.dma_start(dst, src).then_inc(ea_loaded[par], 16)

                    def store_t(j, par, tile):
                        sp.wait_ge(s["t_kept"], 2 * j + 1)
                        flat = trow[:, par, :, :].rearrange("l p k -> l (p k)")
                        if tile is None:
                            rc = -(-REST // P)
                            sp.dma_start(tv[:, NET * KE:NCH, :], flat[:, 0:rc * P].rearrange("l (c e) -> l c e", e=P))\
                                .then_inc(t_stored[par], 16)
                        else:
                            sp.dma_start(tv[:, bass.ds(tile * KE, KE), :], flat.rearrange("l (c e) -> l c e", e=P))\
                                .then_inc(t_stored[par], 16)

                    def load_ti(m_sb, h):
                        sp.dma_start(tirow[:, h, :], tirows[bass.ds(m_sb * G, G), :]).then_inc(ti_loaded[h], 16)

                    def load_rows(m_sb, h, with_t):
                        rows = struct[bass.ds(m_sb * G, G), :]
                        sp.dma_start(strow[:, h, :], rows).then_inc(struct_loaded[h], 16)
                        for f in range(2):
                            sp.dma_start(flags[:, h, f, :], perv[f:f + 1, bass.ds(m_sb * G, G)]).then_inc(struct_loaded[h], 16)
                        if with_t:
                            load_ti(m_sb, h)

                    def store_ti(m_sb, h):
                        sp.wait_ge(s["t_masked"], m_sb + 1)
                        sp.dma_start(tirows[bass.ds(m_sb * G, G), :], tirow[:, h, :]).then_inc(ti_stored[h], 16)

                    sp.dma_start(num, x.rearrange("(t p) d -> p t d", p=P)).then_inc(s["x_loaded"], 16)
                    load_rows(0, 0, False)
                    load_rows(1, 1, False)
                    load_ea(0, 0, PRE[0][1])
                    load_ea(1, 1, PRE[1][1])
                    for k, (j, tile) in enumerate(PRE):
                        sp.wait_ge(s["ea_turned"], 2 * j + 1)
                        nxt = PRE[k + 2][1] if k + 2 < len(PRE) else AHEAD + k + 2 - len(PRE)
                        load_ea(j + 2, j % 2, nxt)
                        if k:
                            store_t(j - 1, (j - 1) % 2, PRE[k - 1][1])
                    sp.wait_ge(s["h_ready"], 1)
                    sp.dma_start(table.rearrange("(t p) f -> p t f", p=P), hbuf[:, :, :]).then_inc(s["table_stored"], 16)
                    with sp.Fori(0, EPAIRS) as pr:
                        for h in range(2):
                            g = 2 * pr + h
                            store_ti(g, h)
                            sp.wait_ge(s["struct_used"], g + 1)
                            load_rows(g + 2, h, False)
                            for k in range(EPS_):
                                tile = AHEAD + g * EPS_ + k
                                j, par = tile + EXTRA + 1, (PI + h * EPS_ + k) % 2
                                sp.wait_ge(s["ea_turned"], 2 * j + 1)
                                load_ea(j + 2, par, tile + 2)
                                store_t(j - 1, 1 - par, tile - 1)
                    store_t(LAST_ITEM, LAST_ITEM % 2, AHEAD + ALONG - 1)
                    with sp.Fori(EPAIRS, NP2 - 1) as pr:
                        for h in range(2):
                            store_ti(2 * pr + h, h)
                            sp.wait_ge(s["struct_used"], 2 * pr + h + 1)
                            load_rows(2 * pr + h + 2, h, False)
                    for h in range(2):
                        store_ti(NSB - 2 + h, h)
                        sp.wait_ge(s["struct_used"], NSB - 2 + h + 1)
                        load_rows(h, h, False)
                    for h in range(2):
                        sp.wait_ge(ti_stored[h], 16 * NP2)
                    for h in range(2):
                        load_ti(h, h)
                    with sp.Fori(1, L) as l:
                        sp.wait_ge(s["h_ready"], l + 1)
                        sp.dma_start(table.rearrange("(t p) f -> p t f", p=P), hbuf[:, :, :]).then_inc(s["table_stored"], 16)
                        with sp.Fori(0, NP2 - 1) as pr:
                            for h in range(2):
                                sp.wait_ge(s["struct_used"], l * NSB + 2 * pr + h + 1)
                                load_rows(2 * pr + h + 2, h, True)
                        for h in range(2):
                            sp.wait_ge(s["struct_used"], l * NSB + NSB - 2 + h + 1)
                            load_rows(h, h, True)
                    sp.wait_ge(s["nodes_ready"], L)
                    sp.dma_start(hbuf[:, :, 0:D], x.rearrange("(t p) d -> p t d", p=P)).then_inc(s["x_again"], 16)
                    sp.wait_ge(s["out_made"], 1)
                    sp.dma_start(out[0:full * P, :].rearrange("(t p) d -> p t d", p=P), num[:, 0:full, :])\
                        .then_inc(s["out_stored"], 16)
                    sp.dma_start(out[full * P:N, :], nodes[0:out_rows, full, 0:D]).then_inc(s["out_stored"], 16)
                    sp.wait_ge(s["out_stored"], 32)
                    for h in range(2):
                        sp.wait_ge(ti_loaded[h], 16 * ((L - 1) * NP2 + 1))
                        sp.wait_ge(struct_loaded[h], 48 * (L * NP2 + 1))
                        sp.wait_ge(t_stored[h], 16 * T_STORES[h])
                        sp.wait_ge(ea_loaded[h], 16 * (T_STORES[h] + 1))

                @block.gpsimd
                def _(pool):
                    p = nc.gpsimd

                    def superblock(g, m_sb, h, fresh_wait):
                        pool.wait_ge(s["slots_free"], g + 1)
                        pool.sem_inc(s["pool_paused"], 1)
                        p.tensor_copy(ixs[:, h, :], idx[:, bass.ds(m_sb * G, G)]).then_inc(s["index_staged"], 1)
                        pool.wait_ge(s["index_staged"], g + 1)
                        pool.sem_inc(s["pool_paused"], 1)
                        for k in range(G):
                            p.indirect_dma_start(ring[:, h * G + k, 0:ROW], None, table,
                                                 bass.IndirectOffsetOnAxis(ixs[:, h, k:k + 1], 0))\
                                .then_inc(gathered[h], 16)
                        if fresh_wait is not None:
                            for b in range(2):
                                pool.wait_ge(t_stored[b], 16 * fresh_wait[b])
                            pool.wait_ge(ti_stored[h], 16 * fresh_wait[2])
                            pool.sem_inc(s["pool_paused"], 1)
                            p.tensor_copy(cvs[:, h:h + 1], cvi[:, bass.ds(m_sb, 1)]).then_inc(s["chunk_staged"], 1)
                            pool.wait_ge(s["chunk_staged"], m_sb + 1)
                            pool.sem_inc(s["pool_paused"], 1)
                            p.indirect_dma_start(tirow[:, h, :], None, tnat, bass.IndirectOffsetOnAxis(cvs[:, h:h + 1], 0))\
                                .then_inc(t_gathered[h], 16)

                    def scale_h(l):
                        pool.wait_ge(s["c_made"], l + 1)
                        p.tensor_tensor(hbuf[:, :, 0:D], hbuf[:, :, 0:D], bc_tile(sm[:, 12, :]), ALU.mult)\
                            .then_inc(s["h_scaled"], 1)

                    pool.wait_ge(s["table_stored"], 16)
                    with pool.Fori(0, EPAIRS) as pr:
                        for h in range(2):
                            g = 2 * pr + h
                            items = (pr * 2 + h + 1) * (EPS_ // 2)
                            superblock(g, g, h, [items + (EXTRA + 2) // 2, items + (EXTRA + 1) // 2, pr])
                    with pool.Fori(EPAIRS, NP2) as pr:
                        for h in range(2):
                            superblock(2 * pr + h, 2 * pr + h, h, T_STORES + [pr])
                    scale_h(0)
                    with pool.Fori(1, L) as l:
                        pool.wait_ge(s["table_stored"], 16 * l + 16)
                        pool.sem_inc(s["pool_paused"], 1)
                        with pool.Fori(0, NP2) as pr:
                            for h in range(2):
                                superblock(l * NSB + 2 * pr + h, 2 * pr + h, h, None)
                        scale_h(l)

                @block.tensor
                def _(pe):
                    t = nc.tensor
                    tiles = [pe.alloc_register(f"tile{k}") for k in range(HG)]

                    def pause():
                        pe.sem_inc(s["pe_paused"], 1)

                    def t_product(c, par, n, p):
                        pe.wait_ge(s["ea_kept"], c + 1)
                        pe.wait_ge(s["t_kept"], c)
                        t.matmul(banks[5][0:L, 0:n * p], vcol[:, :], eat[:, par, 0:n * p], start=True, stop=True)\
                            .then_inc(s["t_made"], 1)

                    def turn_item(j, jpar, loads):
                        pe.wait_ge(ea_loaded[jpar], 16 * loads)
                        for gi in range(NGRP):
                            c = 2 * j - 1 + gi
                            pe.wait_ge(s["ea_kept"], c - 1)
                            for k in range(SUB):
                                last = t.transpose(banks[6 + (1 + gi) % 2][:, k * P:(k + 1) * P],
                                                   ea[:, jpar, gi * SUB + k, :], ident[:, :])
                            last.then_inc(s["ea_turned"], 1)
                            if isinstance(j, int) and c == 1:
                                t_product(0, 0, RK, RP)
                            else:
                                t_product(c - 1, gi % 2, SUB, P)

                    def transform(l):
                        with pe.Fori(0, NT // 7) as ti:
                            for u in range(7):
                                n = l * NT + 7 * ti + u

                                def product(k):
                                    m = l * NT + 7 * ti + k
                                    pe.wait_ge(s["x_turned_kept"], m + 1)
                                    pe.wait_ge(s["h_kept"], m - 1 if k >= 2 else m - k)
                                    t.matmul(banks[3 + k % 2][:, 0:WXW], xt[:, k % 2, :], wx[:, bass.ds(l, 1), :],
                                             start=True, stop=True).then_inc(s["h_made"], 1)
                                pe.wait_ge(s["x_turned_kept"], n - 1 if u >= 2 else n - u)
                                pe.wait_ge(s["x_staged"], n + 1)
                                t.transpose(banks[u % 2][:, 0:P], xs[:, u % 2, :], ident[:, :])\
                                    .then_inc(s["x_turned"], 1)
                                if u:
                                    product(u - 1)
                            product(6)

                    def spread(B, bi, q, hn):
                        b0, n = BATCH[bi]
                        pe.wait_ge(s["hot_t_made"], B - 1 if bi >= 2 else B - bi)
                        for k in range(n):
                            last = t.matmul(banks[bi % 2][:, k * P:(k + 1) * P],
                                            identb[:, bass.ds(q * HG + b0 + k, 1)].broadcast_to([P, P]),
                                            rdb[:, hn, :], start=True, stop=True)
                        last.then_inc(s["spread"], 1)

                    def pick(B, bi, taken=None):
                        b0, n = BATCH[bi]
                        pe.wait_ge(s["hot_t_made"], B + 1)
                        if bi == 0:
                            pe.wait_ge(s["d_taken"], taken)
                        for k in range(n):
                            tile = pe.snap(tiles[b0 + k], min_val=0, max_val=NT - 1)
                            last = t.matmul(banks[2][:, (b0 + k) * 3:(b0 + k) * 3 + 3], hot_t[:, bi % 2, k * P:(k + 1) * P],
                                            dsplit[:, bass.ds(tile, 1), :], start=True, stop=True)
                        last.then_inc(s["d_picked"], 1)

                    def superblock(l, pr, h, edges):
                        g = l * NSB + 2 * pr + h
                        nxt = (2 * pr + h + 1) * G
                        pe.wait_ge(s["logits_cols"], g + 1)
                        if edges:
                            pe.wait_ge(s["ea_kept"], 2 * (AHEAD + (2 * pr + h) * EPS_ + EXTRA + 1) - 1)
                        pause()
                        t.transpose(banks[6][0:G, 0:P], scol[:, :], ident[:, :]).then_inc(s["logits_rows"], 1)
                        pe.wait_ge(s["prefix_max"], g + 1)
                        pause()
                        t.transpose(banks[7][0:1, 0:G], fmax[:, P - 1:P], ident[0:G, 0:G]).then_inc(s["tails_row"], 1)
                        pe.wait_ge(s["carry_row"], g + 1)
                        pause()
                        t.transpose(banks[6][0:G, 0:1], crow[:, h, 0:G], ident[0:1, 0:1]).then_inc(s["carry_cols"], 1)
                        pe.wait_ge(s["suffix_max"], g + 1)
                        pause()
                        t.transpose(banks[7][0:1, 0:G], bmax[:, 0:1], ident[0:G, 0:G]).then_inc(s["heads_row"], 1)
                        pe.wait_ge(s["back_row"], g + 1)
                        pause()
                        t.transpose(banks[6][0:G, 0:1], brow[:, h, 1:G + 1], ident[0:1, 0:1]).then_inc(s["back_cols"], 1)
                        pe.wait_ge(s["w_rows"], g + 1)
                        pe.wait_ge(s["maxima_made"], g + 1)
                        pause()
                        t.transpose(banks[7][:, 0:G], wrow[:, :], ident[0:G, 0:G])
                        t.transpose(banks[7][:, G:2 * G], lastmax[:, :], ident[0:G, 0:G])
                        for k in range(L):
                            last = t.transpose(banks[7][:, (2 + k) * G:(3 + k) * G], tirow[:, h, k * P:(k + 1) * P],
                                               ident[0:G, 0:G])
                        last.then_inc(s["w_cols"], 1)
                        pe.wait_ge(s["w_cols"], g + 1)
                        pe.sem_inc(s["struct_used"], 1)
                        pe.wait_ge(s["carry_factor"], g + 1)
                        t.matmul(banks[6][:, 0:1], ones_row[:, :], drop[:, 1:2], start=True, stop=True)\
                            .then_inc(s["factor_spread"], 1)
                        pe.wait_ge(s["rd_rows"], g + 2)
                        if edges:
                            pe.wait_ge(s["fcol_made"], g + 1)
                        pause()
                        with pe.Fori(0, 2) as q:
                            t.load(tiles, ntile[0:1, bass.ds(nxt + q * HG, HG)])
                            for bi, (b0, n) in enumerate(BATCH):
                                B = l * DLAYER + (2 * pr + h + 1) * DSB + q * NBT + bi
                                spread(B, bi, q, 1 - h)
                                for u in range(b0, b0 + n):
                                    gv = (g * 2 + q) * HG + u
                                    pe.wait_ge(s["hot_made"], gv + 1)
                                    pe.wait_ge(s["weighted"], gv + 1)
                                    pe.wait_ge(s["acc_done"], gv - 1 if u >= 2 else gv - u)
                                    t.matmul(banks[3 + u % 2][:, 0:SLOT], hot[:, u % 4, :],
                                             ring[:, bass.ds(h * G + q * HG + u, 1), :], start=True, stop=True)\
                                        .then_inc(s["summed"], 1)
                                if bi:
                                    pick(B - 1, bi - 1, l * 2 * (NSB + 1) + (2 * pr + h + 1) * 2 + q)
                                if edges:
                                    j = J0 + (2 * pr + h) * EPS_ + q * (EPS_ // 2) + bi // 2
                                    c = 2 * j - 1 + bi % 2
                                    jp = (J0 + bi // 2) % 2
                                    if bi % 2 == 0:
                                        pe.wait_ge(ea_loaded[jp], 16 * ((2 * pr + h) * (EPS_ // 2) + q * (EPS_ // 4)
                                                                        + (J0 + bi // 2) // 2 + 1))
                                    pe.wait_ge(s["ea_kept"], c - 1)
                                    for k in range(SUB):
                                        last = t.transpose(banks[6 + (1 + bi) % 2][:, k * P:(k + 1) * P],
                                                           ea[:, jp, (bi % 2) * SUB + k, :], ident[:, :])
                                    last.then_inc(s["ea_turned"], 1)
                                    t_product(c - 1, bi % 2, SUB, P)
                            B = l * DLAYER + (2 * pr + h + 1) * DSB + q * NBT + NBT - 1
                            pick(B, NBT - 1)
                        pe.wait_ge(s["summed"], (g + 1) * G)
                        pe.sem_inc(s["slots_free"], 1)

                    pe.sem_inc(s["slots_free"], 2)
                    pe.wait_ge(ea_loaded[0], 16)
                    for k in range(RK):
                        last = t.transpose(banks[6][:, k * RP:(k + 1) * RP], ea[0:RP, 0, k, :], ident[0:RP, 0:RP])
                    last.then_inc(s["ea_turned"], 1)
                    for j in range(1, EXTRA + 1):
                        turn_item(j, j % 2, j // 2 + 1)
                    with pe.Fori(0, AHEAD // 2) as i:
                        for k in range(2):
                            j = item_of_tile(0) + k
                            turn_item(j + 2 * i, j % 2, j // 2 + 1 + i)
                    pe.wait_ge(s["x_loaded"], 16)

                    def layer_start(l):
                        transform(l)
                        pe.wait_ge(s["rd_rows"], l * NSB + 1)
                        pause()
                        with pe.Fori(0, 2) as q:
                            t.load(tiles, ntile[0:1, bass.ds(q * HG, HG)])
                            for bi in range(NBT):
                                B = l * DLAYER + q * NBT + bi
                                spread(B, bi, q, 0)
                                if bi:
                                    pick(B - 1, bi - 1, l * 2 * (NSB + 1) + q)
                            pick(l * DLAYER + q * NBT + NBT - 1, NBT - 1)

                    layer_start(0)
                    with pe.Fori(0, EPAIRS) as pr:
                        for h in range(2):
                            superblock(0, pr, h, True)
                    t_product(2 * LAST_ITEM, 0, SUB, P)
                    with pe.Fori(EPAIRS, NP2) as pr:
                        for h in range(2):
                            superblock(0, pr, h, False)
                    with pe.Fori(1, L) as l:
                        pe.wait_ge(s["nodes_ready"], l)
                        pause()
                        layer_start(l)
                        with pe.Fori(0, NP2) as pr:
                            for h in range(2):
                                superblock(l, pr, h, False)

                @block.scalar
                def _(act):
                    a = nc.scalar

                    def keep_turned(c, cpar, n, p):
                        act.wait_ge(s["ea_turned"], c + 1)
                        if not isinstance(c, int) or c >= 1:
                            act.wait_ge(s["t_made"], c - 1)
                        a.activation(eat[:, cpar, 0:n * p], banks[6 + cpar][:, 0:n * p], ACT.Copy)\
                            .then_inc(s["ea_kept"], 1)

                    def keep_t(c, j, jpar, gi, stores, n=SUB, p=P, k=KE):
                        act.wait_ge(s["t_made"], c + 1)
                        if gi == 0:
                            act.wait_ge(t_stored[jpar], 16 * stores)
                        row = trow[:, jpar, :, :].rearrange("l p k -> l (p k)")[:, 0:p * k].rearrange("l (p k) -> l k p", k=k)
                        a.activation(row[:, gi * SUB:gi * SUB + n, :],
                                     banks[5][0:L, 0:n * p].rearrange("l (k p) -> l k p", p=p), ACT.Copy)\
                            .then_inc(s["t_kept"], 1)

                    def item(j, jpar, half):
                        c = 2 * j - 1
                        keep_turned(c, 1, SUB, P)
                        if isinstance(j, int) and j == 1:
                            keep_t(0, 0, 0, 0, 0, RK, RP, RK)
                        else:
                            keep_t(c - 1, j - 1, 1 - jpar, 1, None)
                        keep_turned(c + 1, 0, SUB, P)
                        keep_t(c, j, jpar, 0, half)

                    def transform(l):
                        with act.Fori(0, NT // 7) as ti:
                            def stage(k):
                                m = l * NT + 7 * ti + k
                                act.wait_ge(s["x_turned"], m - 1 if k >= 2 else m - k)
                                a.activation(xs[:, k % 2, :], nodes[:, bass.ds(7 * ti + k, 1), 0:D], ACT.Copy)\
                                    .then_inc(s["x_staged"], 1)
                            stage(0)
                            for u in range(7):
                                n = l * NT + 7 * ti + u
                                if u < 6:
                                    stage(u + 1)
                                act.wait_ge(s["x_turned"], n + 1)
                                act.wait_ge(s["h_made"], n - 1 if u >= 2 else n - u)
                                a.activation(xt[:, u % 2, :], banks[u % 2][:, 0:P], ACT.Copy).then_inc(s["x_turned_kept"], 1)

                    def superblock(l, pr, h, edges):
                        g = l * NSB + 2 * pr + h
                        act.wait_ge(s["diff_made"], g + 1)
                        a.activation(wrow[:, :], diff[:, :], ACT.Exp).then_inc(s["w_rows"], 1)
                        act.wait_ge(s["carry_drop"], g + 1)
                        a.activation(drop[:, 1:2], drop[:, 0:1], ACT.Exp).then_inc(s["carry_factor"], 1)
                        act.wait_ge(s["weights_ready"], g + 1)
                        act.sem_inc(s["act_paused"], 1)
                        with act.Fori(0, 2) as q:
                            for bi, (b0, n) in enumerate(BATCH):
                                for u in range(b0, b0 + n):
                                    slot = ring[:, bass.ds(h * G + q * HG + u, 1), 0:D + 1]
                                    a.activation(slot, slot, ACT.Copy, scale=wcol[:, h, bass.ds(q * HG + u, 1)])\
                                        .then_inc(s["weighted"], 1)
                                if edges:
                                    base = (2 * pr + h) * EPS_ + q * (EPS_ // 2)
                                    half = (2 * pr + h) * (EPS_ // 2) + q * (EPS_ // 4) + (J0 + bi // 2) // 2
                                    j = J0 + base + bi // 2
                                    jp = (J0 + bi // 2) % 2
                                    c = 2 * j - 1 + bi % 2
                                    keep_turned(c, (1 + bi) % 2, SUB, P)
                                    if bi % 2 == 0:
                                        keep_t(c - 1, j - 1, 1 - jp, 1, None)
                                    else:
                                        keep_t(c - 1, j, jp, 0, half)

                    def loop_over_self(l):
                        act.wait_ge(s["f_made"], l + 1)
                        a.activation(sm[:, 8:10, :], sm[:, 6:8, :], ACT.Exp).then_inc(s["f_exp"], 1)

                    def normalise(count):
                        act.wait_ge(s["centred"], count)
                        a.activation(hbuf[:, :, 0:D], num, ACT.Square).then_inc(s["squared"], 1)
                        act.wait_ge(s["var_made"], count)
                        a.activation(sm[:, 14, :], sm[:, 13, :], ACT.Sqrt).then_inc(s["std_made"], 1)

                    act.wait_ge(s["base_set"], 4)
                    keep_turned(0, 0, RK, RP)
                    for j in range(1, EXTRA + 1):
                        item(j, j % 2, j // 2)
                    with act.Fori(0, AHEAD // 2) as i:
                        for k in range(2):
                            j = item_of_tile(0) + k
                            item(j + 2 * i, j % 2, j // 2 + i)
                    act.wait_ge(s["x_loaded"], 16)
                    transform(0)
                    with act.Fori(0, EPAIRS) as pr:
                        for h in range(2):
                            superblock(0, pr, h, True)
                    keep_t(2 * LAST_ITEM, LAST_ITEM, LAST_ITEM % 2, 1, None)
                    with act.Fori(EPAIRS, NP2) as pr:
                        for h in range(2):
                            superblock(0, pr, h, False)
                    loop_over_self(0)
                    normalise(1)
                    with act.Fori(1, L) as l:
                        act.wait_ge(s["nodes_ready"], l)
                        act.sem_inc(s["act_paused"], 1)
                        transform(l)
                        with act.Fori(0, NP2) as pr:
                            for h in range(2):
                                superblock(l, pr, h, False)
                        loop_over_self(l)
                        normalise(l + 1)
                    normalise(L + 1)

                @block.vector
                def _(dve):
                    v = nc.vector
                    VR = 4 * (-(-HG // 8))
                    tiles = [dve.alloc_register(f"vtile{k}") for k in range(VR)]
                    SB_LINKS, TOP_LINKS, END_LINKS = 7, 6, 23
                    PER_LAYER = TOP_LINKS + END_LINKS + NSB * SB_LINKS

                    def normalise(count, link, last):
                        link(v.tensor_reduce(sm[:, 13, :], num, AX.X, ALU.add))
                        link(v.tensor_scalar(sm[:, 13, :], sm[:, 13, :], 1.0 / D, None, ALU.mult))
                        v.tensor_tensor(num, num, bc_tile(sm[:, 13, :]), ALU.subtract).then_inc(s["centred"], 1)
                        dve.wait_ge(s["squared"], count)
                        link(v.tensor_reduce(sm[:, 13, :], hbuf[:, :, 0:D], AX.X, ALU.add))
                        v.tensor_scalar(sm[:, 13, :], sm[:, 13, :], 1.0 / D, LN_EPS, ALU.mult, ALU.add)\
                            .then_inc(s["var_made"], 1)
                        dve.wait_ge(s["std_made"], count)
                        link(v.reciprocal(sm[:, 15, :], sm[:, 14, :]))
                        last(v.tensor_tensor(num, num, bc_tile(sm[:, 15, :]), ALU.mult))

                    def turn_hot(B, bi):
                        n = BATCH[bi][1]
                        dve.wait_ge(s["spread"], B + 1)
                        dve.wait_ge(s["d_picked"], B - 1 if bi >= 2 else B - bi)
                        v.tensor_scalar(hot_t[:, bi % 2, 0:n * P], banks[bi % 2][:, 0:n * P],
                                        iota_col[:, :], None, ALU.is_equal).then_inc(s["hot_t_made"], 1)

                    def take_d(B_end, q, hn):
                        dve.wait_ge(s["d_picked"], B_end)
                        v.tensor_reduce(dedge[:, hn, bass.ds(q * HG, HG)],
                                        banks[2][:, 0:3 * HG].rearrange("p (v c) -> p v c", c=3),
                                        AX.X, ALU.add).then_inc(s["d_taken"], 1)

                    def layer_start(l):
                        with dve.Fori(0, NT // 7) as ti:
                            for u in range(7):
                                n = l * NT + 7 * ti + u
                                dve.wait_ge(s["h_made"], n + 1)
                                v.tensor_copy(hbuf[:, bass.ds(7 * ti + u, 1), :], banks[3 + u % 2][:, 0:ROW])
                                v.tensor_copy(dnode[:, bass.ds(7 * ti + u, 1)], banks[3 + u % 2][:, D + 2:D + 3])\
                                    .then_inc(s["h_kept"], 1)
                        dve.wait_ge(s["h_kept"], (l + 1) * NT)
                        v.memset(hbuf[:, :, C_ONE], 1.0).then_inc(s["h_ready"], 1)
                        link = Chain(dve, s["dve_links"], l * PER_LAYER)
                        v.memset(crow[:, 1, G:G + 1], -BIG)
                        link(v.tensor_copy(dsplit[:, :, 0], dnode[:, :]))
                        link(v.tensor_tensor(drest[:, 0, :], dnode[:, :], dsplit[:, :, 0], ALU.subtract))
                        link(v.tensor_copy(dsplit[:, :, 1], drest[:, 0, :]))
                        link(v.tensor_tensor(drest[:, 1, :], drest[:, 0, :], dsplit[:, :, 1], ALU.subtract))
                        link(v.tensor_copy(dsplit[:, :, 2], drest[:, 1, :]))
                        link(v.memset(nodes[:, :, :], 0.0))
                        assert link.n == TOP_LINKS
                        dve.sem_inc(s["dve_paused"], 1)
                        with dve.Fori(0, 2) as q:
                            for bi in range(NBT):
                                turn_hot(l * DLAYER + q * NBT + bi, bi)
                            take_d(l * DLAYER + (q + 1) * NBT, q, 0)

                    def superblock(l, pr, h, fresh):
                        g = l * NSB + 2 * pr + h
                        pair = l * NP2 + pr + 1
                        first = (2 * pr + h) * G
                        link = Chain(dve, s["dve_links"], l * PER_LAYER + TOP_LINKS + (2 * pr + h) * SB_LINKS)
                        field = {f: strow[:, h, f * P:(f + 1) * P] for f in range(NFIELD)}
                        link(v.tensor_copy(crow[:, h, 0:1], crow[:, 1 - h, G:G + 1]))
                        dve.wait_ge(struct_loaded[1 - h], 48 * (pair + h))
                        v.tensor_copy(rdb[0:G, 1 - h, :], strow[:, 1 - h, S_RD * P:(S_RD + 1) * P]).then_inc(s["rd_rows"], 1)
                        if fresh:
                            v.tensor_scalar(outside[:, :], field[S_RD], 0.0, -BIG, ALU.is_lt, ALU.mult)\
                                .then_inc(s["outside_made"], 1)
                            dve.wait_ge(s["outside_made"], g + 1)
                        dve.wait_ge(s["d_taken"], l * 2 * (NSB + 1) + (2 * pr + h + 1) * 2)
                        dve.wait_ge(gathered[h], 16 * G * pair)
                        v.tensor_tensor(scol[:, :], ring[:, h * G:(h + 1) * G, C_S], dedge[:, h, :], ALU.add)\
                            .then_inc(s["logits_cols"], 1)
                        if fresh:
                            dve.wait_ge(t_gathered[h], 16 * pair)
                            ti = tirow[:, h, :].rearrange("g (l e) -> g l e", l=L)
                            v.tensor_tensor(ti, ti, outside[:, :].unsqueeze(1).broadcast_to([G, L, P]), ALU.add)\
                                .then_inc(s["t_masked"], 1)
                            dve.wait_ge(s["t_masked"], g + 1)
                            t_row = tirow[:, h, 0:P]
                        else:
                            dve.wait_ge(ti_loaded[h], 16 * (pair - NP2))
                            t_row = tirow[:, h, bass.ds(l * P, P)]
                        dve.wait_ge(s["logits_rows"], g + 1)
                        link(v.tensor_tensor(logit_u[:, :], banks[6][0:G, 0:P], t_row, ALU.add))
                        link(v.scalar_tensor_tensor(logit[:, :], logit_u[:, :], SLOPE, logit_u[:, :], ALU.mult, ALU.max))
                        v.tensor_tensor_scan(fmax[:, :], field[S_RF], logit[:, :], -BIG, ALU.add, ALU.max)\
                            .then_inc(s["prefix_max"], 1)
                        dve.wait_ge(s["tails_row"], g + 1)
                        v.tensor_tensor_scan(crow[:, h, 1:G + 1], flags[:, h, 0, :], banks[7][0:1, 0:G],
                                             crow[:, h, 0:1], ALU.add, ALU.max).then_inc(s["carry_row"], 1)
                        dve.wait_ge(s["carry_cols"], g + 1)
                        link(v.scalar_tensor_tensor(fmax2[:, :], field[S_OF], banks[6][0:G, 0:1], fmax[:, :],
                                                    ALU.add, ALU.max))
                        v.tensor_tensor_scan(bmax[:, ::-1], field[S_RB][:, ::-1], fmax2[:, ::-1], -BIG,
                                             ALU.add, ALU.max).then_inc(s["suffix_max"], 1)
                        dve.wait_ge(s["heads_row"], g + 1)
                        v.tensor_tensor_scan(brow[:, h, 0:G][:, ::-1], flags[:, h, 1, :][:, ::-1],
                                             banks[7][0:1, 0:G][:, ::-1], -BIG, ALU.add, ALU.max)\
                            .then_inc(s["back_row"], 1)
                        dve.wait_ge(s["back_cols"], g + 1)
                        link(v.scalar_tensor_tensor(segmax[:, :], field[S_OB], banks[6][0:G, 0:1], bmax[:, :],
                                                    ALU.add, ALU.max))
                        v.tensor_tensor(diff[:, :], logit[:, :], segmax[:, :], ALU.subtract).then_inc(s["diff_made"], 1)
                        v.scalar_tensor_tensor(lastmax[:, :], field[S_RB], -1.0 / BIG, segmax[:, :],
                                               ALU.mult, ALU.mult).then_inc(s["maxima_made"], 1)
                        dve.wait_ge(s["back_row"], g + 1)
                        link(v.tensor_tensor(drop[:, 0:1], crow[:, h, 0:1], brow[:, h, 0:1], ALU.subtract))
                        v.tensor_scalar(drop[:, 0:1], drop[:, 0:1], 0.0, None, ALU.min).then_inc(s["carry_drop"], 1)
                        v.load(tiles[0:1], ntile[0:1, bass.ds(first, 1)])
                        dve.wait_ge(s["w_cols"], g + 1)
                        v.tensor_copy(wcol[:, h, :], banks[7][:, 0:G])
                        v.tensor_copy(ring[:, h * G:(h + 1) * G, C_M:C_T + L].rearrange("p v c -> p c v"),
                                      banks[7][:, G:(2 + L) * G].rearrange("p (c v) -> p c v", c=1 + L))\
                            .then_inc(s["weights_ready"], 1)
                        dve.wait_ge(s["factor_spread"], g + 1)
                        v.scalar_tensor_tensor(fcol[:, :], carry_hot[:, bass.ds(2 * pr + h, 1)], banks[6][:, 0:1],
                                               carry_not[:, bass.ds(2 * pr + h, 1)], ALU.mult, ALU.add)\
                            .then_inc(s["fcol_made"], 1)
                        dve.wait_ge(s["fcol_made"], g + 1)
                        dve.wait_ge(s["acc_done"], g * G)
                        tile = dve.snap(tiles[0], min_val=0, max_val=NT - 1)
                        own = nodes[:, bass.ds(tile, 1), 0:D + 1]
                        link(v.tensor_scalar(own, own, fcol[:, :], None, ALU.mult))
                        assert link.n == SB_LINKS, link.n
                        dve.sem_inc(s["dve_paused"], 1)

                        with dve.Fori(0, 2) as q:
                            def accumulate(u):
                                if u % VR == 0:
                                    some = min(VR, HG - u)
                                    v.load(tiles[0:some], ntile[0:1, bass.ds(first + q * HG + u, some)])
                                gv = (g * 2 + q) * HG + u
                                dve.wait_ge(s["summed"], gv + 1)
                                dve.wait_ge(s["acc_done"], gv)
                                tile = dve.snap(tiles[u % VR], min_val=0, max_val=NT - 1)
                                own = nodes[:, bass.ds(tile, 1), :]
                                v.tensor_tensor(own, own, banks[3 + u % 2][:, 0:SLOT], ALU.add)\
                                    .then_inc(s["acc_done"], 1)
                            for bi, (b0, n) in enumerate(BATCH):
                                for u in range(b0, b0 + n):
                                    v.tensor_scalar(hot[:, u % 4, :], iota_row[:, :],
                                                    rdcol[:, bass.ds(first + q * HG + u, 1)], None, ALU.is_equal)\
                                        .then_inc(s["hot_made"], 1)
                                    if u >= 2:
                                        accumulate(u - 2)
                                turn_hot(l * DLAYER + (2 * pr + h + 1) * DSB + q * NBT + bi, bi)
                            accumulate(HG - 2)
                            accumulate(HG - 1)
                            take_d(l * DLAYER + (2 * pr + h + 1) * DSB + (q + 1) * NBT, q, 1 - h)

                    def layer_end(l):
                        link = Chain(dve, s["dve_links"], l * PER_LAYER + TOP_LINKS + NSB * SB_LINKS)
                        dve.wait_ge(s["acc_done"], (l + 1) * NV)
                        cnt = nodes[:, :, C_CNT]
                        tsum = nodes[:, :, bass.ds(C_T + l, 1)].rearrange("p t o -> p (t o)")
                        link(v.tensor_scalar(sm[:, 0, :], cnt, 1.0, None, ALU.max))
                        link(v.reciprocal(sm[:, 1, :], sm[:, 0, :]))
                        link(v.tensor_tensor(sm[:, 2, :], tsum, sm[:, 1, :], ALU.mult))
                        link(v.tensor_tensor(sm[:, 2, :], sm[:, 2, :], hbuf[:, :, C_S], ALU.add))
                        link(v.tensor_tensor(sm[:, 2, :], sm[:, 2, :], dnode[:, :], ALU.add))
                        link(v.scalar_tensor_tensor(sm[:, 3, :], sm[:, 2, :], SLOPE, sm[:, 2, :], ALU.mult, ALU.max))
                        link(v.tensor_scalar(sm[:, 4, :], cnt, 0.0, -BIG, ALU.is_equal, ALU.mult))
                        link(v.tensor_tensor(sm[:, 4, :], sm[:, 4, :], nodes[:, :, C_M], ALU.add))
                        link(v.tensor_tensor(sm[:, 5, :], sm[:, 4, :], sm[:, 3, :], ALU.max))
                        link(v.tensor_tensor(sm[:, 6, :], sm[:, 4, :], sm[:, 5, :], ALU.subtract))
                        v.tensor_tensor(sm[:, 7, :], sm[:, 3, :], sm[:, 5, :], ALU.subtract).then_inc(s["f_made"], 1)
                        dve.wait_ge(s["f_exp"], l + 1)
                        link(v.tensor_tensor(sm[:, 10, :], nodes[:, :, C_ONE], sm[:, 8, :], ALU.mult))
                        link(v.tensor_tensor(sm[:, 10, :], sm[:, 10, :], sm[:, 9, :], ALU.add))
                        link(v.reciprocal(sm[:, 11, :], sm[:, 10, :]))
                        v.tensor_tensor(sm[:, 12, :], sm[:, 9, :], sm[:, 11, :], ALU.mult).then_inc(s["c_made"], 1)
                        link(v.tensor_tensor(sm[:, 11, :], sm[:, 8, :], sm[:, 11, :], ALU.mult))
                        link(v.tensor_tensor(num, num, bc_tile(sm[:, 11, :]), ALU.mult))
                        dve.wait_ge(s["h_scaled"], l + 1)
                        link(v.tensor_tensor(num, num, hbuf[:, :, 0:D], ALU.add))

                        def param(c):
                            return par[:, bass.ds(l, 1), c, :].broadcast_to([P, NT, D])
                        link(v.tensor_tensor(num, num, param(0), ALU.add))
                        normalise(l + 1, link, link)
                        link(v.tensor_tensor(num, num, param(1), ALU.mult))
                        assert link.n == END_LINKS, link.n
                        v.tensor_tensor(num, num, param(2), ALU.add).then_inc(s["nodes_ready"], 1)

                    v.memset(rdb[:, :, :], 0.0).then_inc(s["base_set"], 1)
                    v.memset(ring[:, :, C_CNT], 1.0).then_inc(s["base_set"], 1)
                    v.memset(brow[:, :, G:G + 1], -BIG).then_inc(s["base_set"], 1)
                    v.memset(trow[:, :, :, :], 0.0).then_inc(s["base_set"], 1)
                    dve.wait_ge(s["base_set"], 4)
                    dve.wait_ge(struct_loaded[0], 48)
                    v.tensor_copy(rdb[0:G, 0, :], strow[:, 0, S_RD * P:(S_RD + 1) * P]).then_inc(s["rd_rows"], 1)
                    layer_start(0)
                    with dve.Fori(0, NP2) as pr:
                        for h in range(2):
                            superblock(0, pr, h, True)
                    layer_end(0)
                    with dve.Fori(1, L) as l:
                        layer_start(l)
                        with dve.Fori(0, NP2) as pr:
                            for h in range(2):
                                superblock(l, pr, h, False)
                        layer_end(l)
                    link = Chain(dve, s["dve_links"], L * PER_LAYER)
                    dve.wait_ge(s["x_again"], 16)
                    dve.wait_ge(s["nodes_ready"], L)
                    link(v.tensor_tensor(num, num, hbuf[:, :, 0:D], ALU.add))
                    normalise(L + 1, link, lambda ins: ins.then_inc(s["out_made"], 1))


def kernel(x, src, dst, edge_attr_128, L0_gnn_W, L0_gnn_att_src, L0_gnn_att_dst, L0_gnn_W_e,
           L0_gnn_att_edge, L0_gnn_bias, L0_gnn_ln_gamma, L0_gnn_ln_beta):
    import concourse.bacc as bacc
    from concourse.bass_utils import run_bass_kernel_spmd as run

    xp = np.zeros((NT * P, D), np.float32)
    xp[:N] = np.asarray(x)
    d = np.full(NCH * P + 2, 1 << 20, np.int32)
    d[0] = -1
    d[1:E + 1] = np.asarray(dst)
    s = np.zeros(NCH * P, np.int32)
    s[:E] = np.asarray(src)
    ei = np.empty((NCH, EIW), np.int32)
    for k in range(P + 2):
        ei[:, k] = d[k:k + (NCH - 1) * P + 1:P]
    ei[:, P + 2:] = s.reshape(NCH, P)
    last = np.full(NCH, N - 1, np.int32)
    last[:NCH - 1] = np.asarray(dst)[P - 1::P][:NCH - 1]
    att = np.empty((D, 3 * L), np.float32)
    for l in range(L):
        att[:, 3 * l] = np.asarray(L0_gnn_att_src)[l]
        att[:, 3 * l + 1] = np.asarray(L0_gnn_att_dst)[l]
        att[:, 3 * l + 2] = np.asarray(L0_gnn_att_edge)[l]
    par = np.stack([np.asarray(L0_gnn_bias), np.asarray(L0_gnn_ln_gamma), np.asarray(L0_gnn_ln_beta)], 1).reshape(-1)
    w = np.asarray(L0_gnn_W)
    arrays = {
        "x": xp, "ei": ei, "chunk_last": last, "edge_attr": np.ascontiguousarray(edge_attr_128),
        "w": np.ascontiguousarray(w), "wt": np.ascontiguousarray(w.transpose(0, 2, 1)),
        "wet": np.ascontiguousarray(np.asarray(L0_gnn_W_e).transpose(0, 2, 1)), "att": att, "params": par,
    }
    nc = bacc.Bacc("TRN2", target_bir_lowering=False, num_devices=1)
    args = [nc.dram_tensor(f"in_{n}", a.shape, mybir.dt.from_np(a.dtype), kind="ExternalInput").ap()
            for n, a in arrays.items()]
    args.append(nc.dram_tensor("out_0", (N, D), FP32, kind="ExternalOutput").ap())
    build(nc, *args)
    r = run(nc, [{f"in_{n}": a for n, a in arrays.items()}], core_ids=[0])
    return r.results[0]["out_0"]
```

```python
import numpy as np
import concourse.bass as bass
from concourse import mybir
from contextlib import ExitStack

FP32 = mybir.dt.float32
INT32 = mybir.dt.int32
BF16 = mybir.dt.bfloat16
ALU = mybir.AluOpType
ACT = mybir.ActivationFunctionType
AX = mybir.AxisListType

P = 128
N, E, D, L = 6250, 200000, 128, 3
NT = -(-N // P)
NCH = -(-E // P)
NVIS = NCH + NT - 1
NSB = -(-NVIS // 64)
NSB += NSB % 2
G = -(-NVIS // NSB)
G += G % 2
HG = G // 2
NV = NSB * G
BIG = 2.0 ** 100
LN_EPS = 1e-5
SLOPE = 0.2

C_ONE, C_S, C_M, C_T, C_CNT = D, D + 1, D + 1, D + 2, D + 2 + L
ROW = D + 2
SLOT = C_CNT + 1
S_RF, S_RB, S_OF, S_OB, S_RD = range(5)
NFIELD = 5
EIW = P + 2 + P

KE = 8
ET = P * KE
NET = E // ET
REST = E - NET * ET
RP = REST // KE
SUB = 4
NGRP = KE // SUB
assert 0 < RP and RP * KE == REST and NGRP == 2
EPS_ = -(-G * P // ET)
EPAIRS = (NET - 2 * EPS_) // (2 * EPS_)
ALONG = EPAIRS * 2 * EPS_
AHEAD = 2 * EPS_
EXTRA = NET - ALONG - AHEAD
NCK = 7
CT = NT // NCK
TB = 4
assert CT * NCK == NT and CT == 7
WXW = D + 3


class Chain:

    def __init__(self, eng, sem, base=0):
        self.eng, self.sem, self.base, self.n = eng, sem, base, 0

    def __call__(self, ins):
        self.n += 1
        ins.then_inc(self.sem, 1)
        self.eng.wait_ge(self.sem, self.base + self.n)


def build(nc, x, ei, chunk_last, edge_attr, w, wt, wet, att, params, out):
    table = nc.dram_tensor("table", (NT * P, ROW), FP32).ap()
    tnat = nc.dram_tensor("tnat", (NCH, L * P), FP32).ap()
    struct = nc.dram_tensor("struct", (NV, NFIELD * P), FP32).ap()
    tirows = nc.dram_tensor("tirows", (NV, L * P), FP32).ap()
    perv = nc.dram_tensor("perv", (2, NV), FP32).ap()
    perv_i = nc.dram_tensor("perv_i", (1, NV), INT32).ap()

    ctx = ExitStack()

    def tensors(stack):
        def sb(name, shape, dt=FP32):
            return stack.enter_context(nc.sbuf_tensor(name, shape, dt))

        def ps(name):
            return stack.enter_context(nc.psum_tensor(name, [P, 512], FP32))

        def sem(name):
            return stack.enter_context(nc.semaphore(name))
        return sb, ps, sem

    with ctx:
        sb, ps_, sem = tensors(ctx)
        banks = [ps_(f"bank{i}") for i in range(8)]
        ident = sb("ident", [P, P])
        identb = sb("identb", [P, P], BF16)
        iota_row = sb("iota_row", [P, P])
        iota_col = sb("iota_col", [P, 1])
        ones_row = sb("ones_row", [1, P])
        idx = sb("idx", [P, NV + 2 * G], INT32)
        rdcol = sb("rdcol", [P, NV])
        carry_hot = sb("carry_hot", [P, NSB])
        carry_not = sb("carry_not", [P, NSB])
        ntile = sb("ntile", [1, NV + G], INT32)
        wx = sb("wx", [P, L, WXW])
        vcol = sb("vcol", [P, L])
        gb = sb("gb", [P, L, 2])
        cvi = sb("cvi", [G, NSB + 2], INT32)
        par = sb("par", [P, L, 3, P])

        with ExitStack() as st:
            sb, ps_, sem = tensors(st)
            cl = sb("cl", [P, NCH], INT32)
            clf = sb("clf", [P, NCH])
            vid = sb("vid", [G, NSB])
            ncol = sb("ncol", [P, 1])
            ndiag = sb("ndiag", [P, NT + 1])
            nrow = sb("nrow", [G, NT + 1])
            cmp = sb("cmp", [G, NSB, NT])
            nv = sb("nv", [G, NSB])
            n128 = sb("n128", [G, NSB])
            cvf = sb("cvf", [G, NSB])
            HS = NSB // 2
            eit = sb("eit", [G, HS, EIW], INT32)
            names = ["rd", "valid", "rf", "rb", "of", "ob", "tmp", "srcf"]
            a = {n: sb(f"a_{n}", [G, HS, P]) for n in names}
            r1 = sb("r1", [1, HS, P])
            r2 = sb("r2", [1, HS, P])
            cb = sb("cb", [1, NSB])
            pv = sb("pv", [NSB, 3, G])
            pvi = sb("pvi", [NSB, G], INT32)
            rowv = sb("rowv", [G, 3, NSB])
            clc = sb("clc", [P, NCH])
            attc = sb("attc", [P, 3 * L])
            wts = sb("wts", [P, 2, L, P])
            ones_g = sb("ones_g", [P, G])
            zeros = sb("zeros", [P, L * P])
            t_cleared = sem("t_cleared")
            dst_loaded = sem("dst_loaded")
            weights_loaded = sem("weights_loaded")
            consts_made = sem("consts_made")
            dve_chain = sem("dve_chain")
            tile_starts = sem("tile_starts")
            starts_spread = sem("starts_spread")
            chunks_known = sem("chunks_known")
            ints_gathered = sem("ints_gathered")
            masks_made = sem("masks_made")
            masks_stored = sem("masks_stored")
            columns_turned = sem("columns_turned")
            columns_kept = sem("columns_kept")
            half_used = sem("half_used")
            carry_found = sem("carry_found")
            carry_spread = sem("carry_spread")
            row_turned = sem("row_turned")
            row_made = sem("row_made")
            row_stored = sem("row_stored")
            row_back = sem("row_back")
            att_applied = sem("att_applied")
            with nc.Block() as block:
                NB = -(-HS // 8)

                @block.scalar
                def _(act):
                    act.wait_ge(consts_made, 8)
                    whole = NCH // P * P
                    act.dma_start(tnat[0:whole, :].rearrange("(c p) f -> p c f", p=P),
                                  zeros[:, :].unsqueeze(1).broadcast_to([P, NCH // P, L * P])).then_inc(t_cleared, 16)
                    act.dma_start(tnat[whole:NCH, :], zeros[0:NCH - whole, :]).then_inc(t_cleared, 16)
                    act.wait_ge(t_cleared, 32)

                @block.sync
                def _(sp):
                    sp.dma_start(cl[:, :], chunk_last.partition_broadcast(P)).then_inc(dst_loaded, 16)
                    sp.dma_start(attc[:, :], att[:, 0:3 * L]).then_inc(weights_loaded, 16)
                    sp.dma_start(gb[:, :, :].rearrange("p l c -> p (l c)"), att[:, 3 * L:5 * L])\
                        .then_inc(weights_loaded, 16)
                    for l in range(L):
                        sp.dma_start(wx[:, l, 0:D], w[l]).then_inc(weights_loaded, 16)
                        sp.dma_start(wts[:, 0, l, :], wt[l]).then_inc(weights_loaded, 16)
                        sp.dma_start(wts[:, 1, l, :], wet[l]).then_inc(weights_loaded, 16)
                    sp.dma_start(par[:, :, :, :].rearrange("p l c d -> p (l c d)"),
                                 params.partition_broadcast(P)).then_inc(weights_loaded, 16)
                    for hh in range(2):
                        rows = struct[hh * HS * G:(hh + 1) * HS * G, :].rearrange("(s r) f -> r s f", r=G)
                        sp.wait_ge(masks_made, hh + 1)
                        for f, n in enumerate(["rf", "rb", "of", "ob", "rd"]):
                            sp.dma_start(rows[:, :, f * P:(f + 1) * P], a[n][:, :, :]).then_inc(masks_stored, 16)
                    sp.wait_ge(row_made, 1)
                    for f in range(2):
                        sp.dma_start(perv[f, :].rearrange("(s r) -> s r", r=G), pv[:, f + 1, :]).then_inc(row_stored, 16)
                    sp.dma_start(perv_i[0, :].rearrange("(s r) -> s r", r=G), pvi[:, :]).then_inc(row_stored, 16)
                    sp.wait_ge(row_stored, 48)
                    sp.dma_start(ntile[:, 0:NV], perv_i).then_inc(row_back, 16)
                    sp.wait_ge(row_back, 16)
                    sp.wait_ge(masks_stored, 16 * 10)

                @block.gpsimd
                def _(pool):
                    nc.gpsimd.iota(iota_row[:, :], [[1, P]], base=0, channel_multiplier=0,
                                   allow_small_or_imprecise_dtypes=True).then_inc(consts_made, 1)
                    nc.gpsimd.iota(iota_col[:, :], [[1, 1]], base=0, channel_multiplier=1,
                                   allow_small_or_imprecise_dtypes=True).then_inc(consts_made, 1)
                    nc.gpsimd.iota(vid[:, :], [[G, NSB]], base=0, channel_multiplier=1,
                                   allow_small_or_imprecise_dtypes=True).then_inc(consts_made, 1)
                    nc.gpsimd.memset(ones_row[:, :], 1.0).then_inc(consts_made, 1)
                    nc.gpsimd.memset(ones_g[:, :], 1.0).then_inc(consts_made, 1)
                    nc.gpsimd.memset(ident[:, :], 0.0).then_inc(consts_made, 1)
                    pool.wait_ge(consts_made, 6)
                    nc.gpsimd.affine_select(out=ident[:, :], in_=ident[:, :], compare_op=ALU.not_equal, fill=1.0,
                                            base=0, pattern=[[-1, P]], channel_multiplier=1).then_inc(consts_made, 1)
                    nc.gpsimd.memset(ntile[:, NV:NV + G], 0)
                    nc.gpsimd.memset(zeros[:, :], 0.0).then_inc(consts_made, 1)
                    pool.wait_ge(chunks_known, 1)
                    for hh in range(2):
                        if hh:
                            pool.wait_ge(half_used, 1)
                        for s in range(HS):
                            c = hh * HS + s
                            nc.gpsimd.indirect_dma_start(
                                eit[:, s, :], None, ei,
                                bass.IndirectOffsetOnAxis(cvi[:, c:c + 1], 0)).then_inc(ints_gathered, 16)

                @block.vector
                def _(dve):
                    v = nc.vector
                    link = Chain(dve, dve_chain)
                    dve.wait_ge(consts_made, 7)
                    link(v.tensor_copy(identb[:, :], ident[:, :]))
                    dve.wait_ge(dst_loaded, 16)
                    link(v.tensor_single_scalar(cl[:, :], cl[:, :], 7, ALU.arith_shift_right))
                    link(v.tensor_copy(clf[:, :], cl[:, :]))
                    link(v.tensor_scalar(clc[:, :], clf[:, :], iota_col[:, :], None, ALU.is_lt))
                    link(v.tensor_reduce(ncol[:, :], clc[:, :], AX.X, ALU.add))
                    link(v.tensor_scalar(ncol[:, :], ncol[:, :], float(NCH - 1), iota_col[:, :], ALU.min, ALU.add))
                    v.tensor_scalar(ndiag[:, :], ident[:, 0:NT + 1], ncol[:, :], None, ALU.mult).then_inc(tile_starts, 1)
                    dve.wait_ge(starts_spread, 1)
                    link(v.tensor_copy(nrow[:, :], banks[0][0:G, 0:NT + 1]))
                    link(v.tensor_tensor(cmp[:, :, :], vid[:, :].unsqueeze(2).broadcast_to([G, NSB, NT]),
                                         nrow[:, 1:NT + 1].unsqueeze(1).broadcast_to([G, NSB, NT]), ALU.is_ge))
                    link(v.tensor_reduce(nv[:, :], cmp[:, :, :], AX.X, ALU.add))
                    link(v.tensor_scalar(n128[:, :], nv[:, :], float(P), None, ALU.mult))
                    link(v.tensor_tensor(cvf[:, :], vid[:, :], nv[:, :], ALU.subtract))
                    link(v.tensor_scalar(rowv[:, 0, :], nv[:, :], float(NT - 1), None, ALU.min))
                    v.tensor_copy(cvi[:, NSB:NSB + 2], cvf[:, 0:2])
                    v.tensor_copy(cvi[:, 0:NSB], cvf[:, :]).then_inc(chunks_known, 1)
                    for hh in range(2):
                        cols = slice(hh * HS, (hh + 1) * HS)
                        dve.wait_ge(ints_gathered, 16 * HS * (hh + 1))
                        if hh:
                            dve.wait_ge(masks_stored, 80)
                            dve.wait_ge(columns_turned, NB)
                        dst = eit[:, :, 1:P + 1]
                        link(v.tensor_tensor(a["rd"][:, :, :], dst,
                                             n128[:, cols].unsqueeze(2).broadcast_to([G, HS, P]), ALU.subtract))
                        link(v.tensor_scalar(a["tmp"][:, :, :], a["rd"][:, :, :], 0.0, None, ALU.is_ge))
                        link(v.scalar_tensor_tensor(a["valid"][:, :, :], a["rd"][:, :, :], float(P), a["tmp"][:, :, :],
                                                    ALU.is_lt, ALU.mult))
                        link(v.scalar_tensor_tensor(a["tmp"][:, :, :], a["rd"][:, :, :], 1.0, a["valid"][:, :, :],
                                                    ALU.add, ALU.mult))
                        link(v.tensor_scalar(a["rd"][:, :, :], a["tmp"][:, :, :], -1.0, None, ALU.add))
                        for n, off in (("rf", 0), ("rb", 2)):
                            link(v.tensor_tensor(a["tmp"][:, :, :], dst, eit[:, :, off:off + P], ALU.not_equal))
                            link(v.scalar_tensor_tensor(a[n][:, :, :], a["tmp"][:, :, :], -BIG, a["valid"][:, :, :],
                                                        ALU.mult, ALU.mult))
                        link(v.tensor_copy(a["srcf"][:, :, :], eit[:, :, P + 2:EIW]))
                        for s in range(HS):
                            v.tensor_tensor_scan(a["of"][:, s, :], a["rf"][:, s, :], a["rf"][:, s, :], 0.0,
                                                 ALU.min, ALU.min)
                            last = v.tensor_tensor_scan(a["ob"][:, s, ::-1], a["rb"][:, s, ::-1], a["rb"][:, s, ::-1],
                                                        0.0, ALU.min, ALU.min)
                        last.then_inc(masks_made, 1)
                        dve.wait_ge(masks_made, hh + 1)
                        link(v.tensor_copy(rowv[:, 1, cols], a["of"][:, :, P - 1]))
                        v.tensor_copy(rowv[:, 2, cols], a["ob"][:, :, 0]).then_inc(half_used, 1)
                        dve.wait_ge(half_used, hh + 1)
                        va = a["valid"][0:1, :, :]
                        link(v.tensor_tensor(r1[:, :, 1:P], va[:, :, 1:P], va[:, :, 0:P - 1], ALU.is_gt))
                        link(v.tensor_copy(r1[:, :, 0:1], va[:, :, 0:1]))
                        link(v.tensor_scalar(r2[:, :, :], a["rf"][0:1, :, :], 0.0, None, ALU.is_equal))
                        link(v.tensor_tensor(r1[:, :, :], r1[:, :, :], r2[:, :, :], ALU.mult))
                        link(v.scalar_tensor_tensor(r2[:, :, :], a["rd"][0:1, :, :], 1.0, r1[:, :, :], ALU.add, ALU.mult))
                        link(v.tensor_reduce(cb[:, cols], r2[:, :, :], AX.X, ALU.add))
                        for b in range(NB):
                            c0 = (hh * HS + b * 8) * G
                            c1 = (hh * HS + min(HS, b * 8 + 8)) * G
                            dve.wait_ge(columns_turned, hh * NB + b + 1)
                            v.tensor_copy(idx[:, c0:c1], banks[2 * b][:, 0:c1 - c0])
                            v.tensor_copy(rdcol[:, c0:c1], banks[2 * b + 1][:, 0:c1 - c0]).then_inc(columns_kept, 1)
                    dve.wait_ge(columns_kept, 2 * NB)
                    v.tensor_copy(idx[:, NV:NV + 2 * G], idx[:, 0:2 * G])
                    v.tensor_scalar(cb[:, :], cb[:, :], -1.0, None, ALU.add).then_inc(carry_found, 1)
                    dve.wait_ge(carry_spread, 1)
                    v.tensor_scalar(carry_hot[:, :], banks[4][:, 0:NSB], iota_col[:, :], None, ALU.is_equal)
                    v.tensor_scalar(carry_not[:, :], banks[4][:, 0:NSB], iota_col[:, :], None, ALU.not_equal)
                    dve.wait_ge(row_turned, 1)
                    link(v.tensor_copy(pv[:, :, :], banks[5][0:NSB, 0:3 * G].rearrange("p (f g) -> p f g", f=3)))
                    v.tensor_copy(pvi[:, :], pv[:, 0, :]).then_inc(row_made, 1)
                    dve.wait_ge(weights_loaded, 16 * (3 * L + 3))
                    dve.wait_ge(att_applied, 1)
                    v.tensor_copy(wx[:, :, D + 1:D + 3], banks[6][:, 0:2 * L].rearrange("p (l c) -> p l c", c=2))
                    v.tensor_copy(vcol[:, :], banks[6][:, 2 * L:3 * L])
                    v.memset(wx[:, :, D:D + 1], 0.0)

                @block.tensor
                def _(pe):
                    t = nc.tensor
                    pe.wait_ge(tile_starts, 1)
                    t.matmul(banks[0][0:G, 0:NT + 1], ones_g[:, :], ndiag[:, :], start=True, stop=True)\
                        .then_inc(starts_spread, 1)
                    for hh in range(2):
                        pe.wait_ge(masks_made, hh + 1)
                        for b in range(NB):
                            if hh:
                                pe.wait_ge(columns_kept, b + 1)
                            for s in range(b * 8, min(HS, b * 8 + 8)):
                                o = (s - b * 8) * G
                                t.transpose(banks[2 * b][:, o:o + G], a["srcf"][:, s, :], ident[0:G, 0:G])
                                last = t.transpose(banks[2 * b + 1][:, o:o + G], a["rd"][:, s, :], ident[0:G, 0:G])
                            last.then_inc(columns_turned, 1)
                    pe.wait_ge(carry_found, 1)
                    t.matmul(banks[4][:, 0:NSB], ones_row[:, :], cb[:, :], start=True, stop=True).then_inc(carry_spread, 1)
                    for f in range(3):
                        last = t.transpose(banks[5][0:NSB, f * G:(f + 1) * G], rowv[:, f, :], ident[0:G, 0:G])
                    last.then_inc(row_turned, 1)
                    pe.wait_ge(weights_loaded, 16 * (3 * L + 3))
                    for l in range(L):
                        for j in range(3):
                            col = 2 * l + j if j < 2 else 2 * L + l
                            last = t.matmul(banks[6][:, col:col + 1], wts[:, j // 2, l, :],
                                            attc[:, 3 * l + j:3 * l + j + 1], start=True, stop=True)
                    last.then_inc(att_applied, 1)


        with ExitStack() as st:
            sb, ps_, sem = tensors(st)
            nodes = sb("nodes", [P, NT, SLOT])
            hbuf = sb("hbuf", [P, NT, ROW])
            ring = sb("ring", [P, 2 * G, SLOT])
            strow = sb("strow", [G, 2, NFIELD * P])
            tirow = sb("tirow", [G, 2, L * P])
            flags = sb("flags", [1, 2, 2, G])
            ixs = sb("ixs", [P, 2, G], INT32)
            cvs = sb("cvs", [G, 2], INT32)
            rdb = sb("rdb", [P, 2, P], BF16)
            hot_t = sb("hot_t", [P, 2, 4 * P], BF16)
            hot = sb("hot", [P, 8, P])
            xs = sb("xs", [P, TB, P])
            xt = sb("xt", [P, TB, P])
            dnode = sb("dnode", [P, NT])
            dsplit = sb("dsplit", [P, NT, 3], BF16)
            drest = sb("drest", [P, 2, NT])
            dedge = sb("dedge", [P, 2, G])
            scol = sb("scol", [P, G])
            wcol = sb("wcol", [P, 2, G])
            logit = sb("logit", [G, P])
            logit_u = sb("logit_u", [G, P])
            fmax = sb("fmax", [G, P])
            fmax2 = sb("fmax2", [G, P])
            bmax = sb("bmax", [G, P])
            segmax = sb("segmax", [G, P])
            lastmax = sb("lastmax", [G, P])
            diff = sb("diff", [G, P])
            wrow = sb("wrow", [G, P])
            outside = sb("outside", [G, P])
            crow = sb("crow", [1, 2, G + 1])
            brow = sb("brow", [1, 2, G + 1])
            drop = sb("drop", [1, 2])
            fcol = sb("fcol", [P, 1])
            sm = sb("sm", [P, 16, NT])
            stats = sb("stats", [P, CT, 6])
            mvg = sb("mvg", [P, CT, 2])
            mv = sb("mv", [P, NT, 2])
            ea = sb("ea", [P, 2, KE, D])
            eat = sb("eat", [P, 2, SUB * P])
            tcol = sb("tcol", [P, 2, L * KE])
            traw = sb("traw", [G, 2, L * P])

            names = ["x_loaded", "nodes_ready", "x_staged", "x_turned", "x_turned_kept", "h_made", "h_kept", "h_ready",
                     "table_stored", "struct_used", "slots_free", "index_staged", "rd_rows", "spread", "hot_t_made",
                     "d_picked", "dve_links", "logits_cols", "logits_rows", "prefix_max", "tails_row", "carry_row",
                     "carry_cols", "suffix_max", "heads_row", "back_row", "back_cols", "diff_made", "maxima_made",
                     "carry_drop", "w_rows", "carry_factor", "w_cols", "factor_spread", "weights_ready", "weighted",
                     "hot_made", "summed", "acc_done", "f_made", "f_exp", "h_scaled", "c_made",
                     "var_made", "std_made", "nodes_cleared", "x_normed", "scaling", "x_beta",
                     "y_normed", "out_by_act", "out_by_dve", "out_stored", "x_again", "base_set",
                     "ea_turned", "ea_kept", "t_made", "t_kept", "t_masked",
                     "chunk_staged", "d_taken", "fcol_made", "outside_made", "act_paused",
                     "pool_paused", "pe_paused", "dve_paused"]
            s = {n: sem("l_" + n) for n in names}
            struct_loaded = [sem("l_struct_loaded0"), sem("l_struct_loaded1")]
            ti_loaded = [sem("l_ti_loaded0"), sem("l_ti_loaded1")]
            ti_stored = [sem("l_ti_stored0"), sem("l_ti_stored1")]
            t_gathered = [sem("l_t_gathered0"), sem("l_t_gathered1")]
            gathered = [sem("l_gathered0"), sem("l_gathered1")]
            ea_loaded = [sem("l_ea_loaded0"), sem("l_ea_loaded1")]
            t_stored = [sem("l_t_stored0"), sem("l_t_stored1")]
            NP2 = NSB // 2
            BATCH = [(q, min(4, HG - q)) for q in range(0, HG, 4)]
            NBT = len(BATCH)
            LEAD = 4
            DSB = 2 * NBT
            DLAYER = (NSB + 1) * DSB
            assert NBT % 2 == 0 and NBT == EPS_ * NGRP // 2
            num = nodes[:, :, 0:D]
            full, out_rows = N // P, N % P
            tflat = tnat.rearrange("c (a b) -> (c a) b", b=L * KE)

            xagain = ring[:, 0:NT, 0:D]
            NORM_ACT = 4

            def group(a, c):
                return a[:, bass.ds(c * CT, CT), 0:D]

            def bc_group(a, c):
                return a[:, bass.ds(c * CT, CT)].unsqueeze(2).broadcast_to([P, CT, D])

            def bc_param(l, c):
                return par[:, bass.ds(l, 1), c, :].broadcast_to([P, CT, D])

            def item_of_tile(i):
                return i + EXTRA + 1
            REST_ITEM, AFTER_REST = 0, 1
            PRE = [(REST_ITEM, None)] + [(1 + k, NET - EXTRA + k) for k in range(EXTRA)] + \
                  [(item_of_tile(i), i) for i in range(AHEAD)]
            LAST_ITEM = item_of_tile(AHEAD + ALONG - 1)
            J0 = item_of_tile(AHEAD)
            assert EXTRA >= 2 and (EPS_ // 2) % 2 == 0

            AT_START = 3

            def reuse(n, u):
                return n - (TB - 2 if u < 3 else TB - 1) + AT_START

            def visit_sum(u):
                return banks[3 + (u // 2) % 2][:, (u % 2) * SLOT:(u % 2 + 1) * SLOT]

            def ea_source(j, tile):
                if tile is None:
                    return (ea[0:RP, 0, :, :].rearrange("p k d -> p (k d)"),
                            edge_attr[NET * ET:E, :].rearrange("(p k) d -> p (k d)", k=KE))
                return (ea[:, j, :, :].rearrange("p k d -> p (k d)"),
                        edge_attr[bass.ds(tile * ET, ET), :].rearrange("(p k) d -> p (k d)", k=KE))

            NITEMS = LAST_ITEM + 1
            T_STORES = [(NITEMS + 1) // 2, NITEMS // 2]

            with nc.Block() as block:

                @block.sync
                def _(sp):
                    def load_ea(j, par, tile):
                        dst, src = ea_source(par, tile)
                        sp.dma_start(dst, src).then_inc(ea_loaded[par], 16)

                    def store_t(j, par, tile):
                        sp.wait_ge(s["t_kept"], 2 * j + 2)
                        if tile is None:
                            sp.dma_start(tflat[NET * P:NET * P + RP, :], tcol[0:RP, par, :]).then_inc(t_stored[par], 16)
                        else:
                            sp.dma_start(tflat[bass.ds(tile * P, P), :], tcol[:, par, :]).then_inc(t_stored[par], 16)

                    def load_ti(m_sb, h):
                        sp.dma_start(tirow[:, h, :], tirows[bass.ds(m_sb * G, G), :]).then_inc(ti_loaded[h], 16)

                    def load_rows(m_sb, h, with_t):
                        rows = struct[bass.ds(m_sb * G, G), :]
                        sp.dma_start(strow[:, h, :], rows).then_inc(struct_loaded[h], 16)
                        for f in range(2):
                            sp.dma_start(flags[:, h, f, :], perv[f:f + 1, bass.ds(m_sb * G, G)]).then_inc(struct_loaded[h], 16)
                        if with_t:
                            load_ti(m_sb, h)

                    def store_ti(m_sb, h):
                        sp.wait_ge(s["t_masked"], L * (m_sb + 1))
                        sp.dma_start(tirows[bass.ds(m_sb * G, G), :], tirow[:, h, :]).then_inc(ti_stored[h], 16)

                    for h in range(2):
                        sp.sem_inc(ti_stored[h], 1)
                    sp.dma_start(num, x.rearrange("(t p) d -> p t d", p=P)).then_inc(s["x_loaded"], 16)
                    load_rows(0, 0, False)
                    load_rows(1, 1, False)
                    load_ea(0, 0, PRE[0][1])
                    load_ea(1, 1, PRE[1][1])
                    sp.wait_ge(s["h_ready"], 1)
                    sp.dma_start(table.rearrange("(t p) f -> p t f", p=P), hbuf[:, :, :]).then_inc(s["table_stored"], 16)
                    for k, (j, tile) in enumerate(PRE):
                        sp.wait_ge(s["ea_turned"], 2 * j + 2)
                        nxt = PRE[k + 2][1] if k + 2 < len(PRE) else AHEAD + k + 2 - len(PRE)
                        load_ea(j + 2, j % 2, nxt)
                        if k:
                            store_t(j - 1, (j - 1) % 2, PRE[k - 1][1])
                    with sp.Fori(0, EPAIRS) as pr:
                        for h in range(2):
                            g = 2 * pr + h
                            store_ti(g, h)
                            sp.wait_ge(s["struct_used"], g + 1)
                            load_rows(g + 2, h, False)
                            for k in range(EPS_):
                                tile = AHEAD + g * EPS_ + k
                                j, par = tile + EXTRA + 1, (J0 + h * EPS_ + k) % 2
                                sp.wait_ge(s["ea_turned"], 2 * j + 2)
                                load_ea(j + 2, par, tile + 2)
                                store_t(j - 1, 1 - par, tile - 1)
                    store_t(LAST_ITEM, LAST_ITEM % 2, AHEAD + ALONG - 1)
                    with sp.Fori(EPAIRS, NP2 - 1) as pr:
                        for h in range(2):
                            store_ti(2 * pr + h, h)
                            sp.wait_ge(s["struct_used"], 2 * pr + h + 1)
                            load_rows(2 * pr + h + 2, h, False)
                    for h in range(2):
                        store_ti(NSB - 2 + h, h)
                        sp.wait_ge(s["struct_used"], NSB - 2 + h + 1)
                        load_rows(h, h, False)
                    for h in range(2):
                        sp.wait_ge(ti_stored[h], 16 * NP2 + 1)
                    for h in range(2):
                        load_ti(h, h)
                    with sp.Fori(1, L) as l:
                        sp.wait_ge(s["h_ready"], l + 1)
                        sp.dma_start(table.rearrange("(t p) f -> p t f", p=P), hbuf[:, :, :]).then_inc(s["table_stored"], 16)
                        with sp.Fori(0, NP2 - 1) as pr:
                            for h in range(2):
                                sp.wait_ge(s["struct_used"], l * NSB + 2 * pr + h + 1)
                                load_rows(2 * pr + h + 2, h, True)
                        for h in range(2):
                            sp.wait_ge(s["struct_used"], l * NSB + NSB - 2 + h + 1)
                            load_rows(h, h, True)
                    sp.wait_ge(s["f_made"], L)
                    sp.dma_start(xagain, x.rearrange("(t p) d -> p t d", p=P)).then_inc(s["x_again"], 16)
                    order = [c for pair in zip(range(NORM_ACT), range(NORM_ACT, NCK)) for c in pair]
                    order += [c for c in range(NCK) if c not in order]
                    for c in order:
                        if c < NORM_ACT:
                            sp.wait_ge(s["out_by_act"], c + 1)
                        else:
                            sp.wait_ge(s["out_by_dve"], c - NORM_ACT + 1)
                        t0, t1 = c * CT, min((c + 1) * CT, full)
                        sp.dma_start(out[t0 * P:t1 * P, :].rearrange("(t p) d -> p t d", p=P), num[:, t0:t1, :])\
                            .then_inc(s["out_stored"], 16)
                        if c == NCK - 1:
                            sp.dma_start(out[full * P:N, :], nodes[0:out_rows, full, 0:D]).then_inc(s["out_stored"], 16)
                    sp.wait_ge(s["out_stored"], 16 * (NCK + 1))
                    for h in range(2):
                        sp.wait_ge(ti_loaded[h], 16 * ((L - 1) * NP2 + 1))
                        sp.wait_ge(struct_loaded[h], 48 * (L * NP2 + 1))
                        sp.wait_ge(t_stored[h], 16 * T_STORES[h])
                        sp.wait_ge(ea_loaded[h], 16 * (T_STORES[h] + 1))

                @block.gpsimd
                def _(pool):
                    p = nc.gpsimd

                    def superblock(l, pr, h, fresh_wait):
                        m_sb = 2 * pr + h
                        g = l * NSB + m_sb
                        pool.wait_ge(s["index_staged"], g + 1)
                        for k in range(G):
                            if k % HG == 0:
                                pool.wait_ge(s["slots_free"], 2 * g + 1 + k // HG)
                                pool.sem_inc(s["pool_paused"], 1)
                            p.indirect_dma_start(ring[:, h * G + k, 0:ROW], None, table,
                                                 bass.IndirectOffsetOnAxis(ixs[:, h, k:k + 1], 0))\
                                .then_inc(gathered[h], 16)
                        if fresh_wait is not None:
                            for b in range(2):
                                pool.wait_ge(t_stored[b], 16 * fresh_wait[b])
                            pool.wait_ge(s["chunk_staged"], m_sb + 1)
                            pool.sem_inc(s["pool_paused"], 1)
                            p.indirect_dma_start(traw[:, h, :], None, tnat, bass.IndirectOffsetOnAxis(cvs[:, h:h + 1], 0))\
                                .then_inc(t_gathered[h], 16)

                    def scale_h(l):
                        pool.wait_ge(s["c_made"], l + 1)
                        pool.sem_inc(s["pool_paused"], 1)
                        with pool.Fori(0, NCK) as c:
                            hs = group(hbuf, c)
                            p.tensor_tensor(hs, hs, bc_group(sm[:, 12, :], c), ALU.mult).then_inc(s["scaling"], 1)
                            pool.wait_ge(s["scaling"], l * NCK + c + 1)
                            pool.sem_inc(s["pool_paused"], 1)
                            p.tensor_tensor(hs, hs, bc_param(l, 0), ALU.add).then_inc(s["h_scaled"], 1)

                    def layer_start(l):
                        if isinstance(l, int):
                            pool.wait_ge(s["x_loaded"], 16)
                            pool.sem_inc(s["pool_paused"], 1)
                        with pool.Fori(0, NT // 7) as ti:
                            if not isinstance(l, int):
                                pool.wait_ge(s["x_normed"], (l - 1) * NCK + ti + 1)
                            for k in range(7):
                                pool.wait_ge(s["x_turned"], reuse(l * NT + 7 * ti + k, k))
                                pool.sem_inc(s["pool_paused"], 1)
                                p.tensor_copy(xs[:, k % TB, :], nodes[:, bass.ds(7 * ti + k, 1), 0:D])\
                                    .then_inc(s["x_staged"], 1)
                        pool.wait_ge(s["x_staged"], (l + 1) * NT)
                        pool.sem_inc(s["pool_paused"], 1)
                        p.memset(nodes[:, :, :], 0.0).then_inc(s["nodes_cleared"], 1)
                        pool.wait_ge(s["table_stored"], 16 * l + 16)
                        pool.sem_inc(s["pool_paused"], 1)

                    layer_start(0)
                    with pool.Fori(0, EPAIRS + 1) as pr:
                        for h in range(2):
                            items = (pr * 2 + h + 1) * (EPS_ // 2)
                            superblock(0, pr, h, [items + (EXTRA + 2) // 2, items + (EXTRA + 1) // 2])
                    with pool.Fori(EPAIRS + 1, NP2) as pr:
                        for h in range(2):
                            superblock(0, pr, h, T_STORES)
                    scale_h(0)
                    with pool.Fori(1, L) as l:
                        layer_start(l)
                        with pool.Fori(0, NP2) as pr:
                            for h in range(2):
                                superblock(l, pr, h, None)
                        scale_h(l)
                    pool.wait_ge(s["x_again"], 16)
                    pool.sem_inc(s["pool_paused"], 1)
                    with pool.Fori(0, NCK) as c:
                        p.tensor_tensor(group(xagain, c), group(xagain, c), bc_param(L - 1, 2), ALU.add)\
                            .then_inc(s["x_beta"], 1)

                @block.tensor
                def _(pe):
                    t = nc.tensor
                    tiles = [pe.alloc_register(f"tile{k}") for k in range(HG)]

                    def pause():
                        pe.sem_inc(s["pe_paused"], 1)

                    def t_product(c, par, p=P):
                        pe.wait_ge(s["ea_kept"], c + 1)
                        pe.wait_ge(s["t_kept"], c)
                        for k in range(SUB):
                            last = t.matmul(banks[5][0:p, k * L:(k + 1) * L], eat[:, par, k * p:(k + 1) * p],
                                            vcol[:, :], start=True, stop=True)
                        last.then_inc(s["t_made"], 1)

                    def turn_group(c, jpar, gi, p=P, p_before=P):
                        if not isinstance(c, int) or c >= 2:
                            pe.wait_ge(s["ea_kept"], c - 1)
                        for k in range(SUB):
                            last = t.transpose(banks[6 + gi][:, k * p:(k + 1) * p],
                                               ea[0:p, jpar, gi * SUB + k, :], ident[0:p, 0:p])
                        last.then_inc(s["ea_turned"], 1)
                        if not isinstance(c, int) or c >= 1:
                            t_product(c - 1, 1 - gi, p_before)

                    def turn_item(j, jpar, loads):
                        pe.wait_ge(ea_loaded[jpar], 16 * loads)
                        rest, after_rest = j is REST_ITEM, j is AFTER_REST
                        for gi in range(NGRP):
                            turn_group(2 * j + gi, jpar, gi, RP if rest else P,
                                       RP if rest or (after_rest and gi == 0) else P)

                    def transform(l):
                        with pe.Fori(0, NT // 7) as ti:
                            for u in range(7):
                                n = l * NT + 7 * ti + u

                                def product(k):
                                    m = l * NT + 7 * ti + k
                                    pe.wait_ge(s["x_turned_kept"], m + 1 + AT_START)
                                    pe.wait_ge(s["h_kept"], reuse(m, k))
                                    t.matmul(banks[TB + k % TB][:, 0:WXW], xt[:, k % TB, :], wx[:, bass.ds(l, 1), :],
                                             start=True, stop=True).then_inc(s["h_made"], 1)
                                pe.wait_ge(s["x_turned_kept"], reuse(n, u))
                                pe.wait_ge(s["x_staged"], n + 1)
                                t.transpose(banks[u % TB][:, 0:P], xs[:, u % TB, :], ident[:, :])\
                                    .then_inc(s["x_turned"], 1)
                                if u:
                                    product(u - 1)
                            product(6)
                        pe.wait_ge(s["h_kept"], (l + 1) * NT + AT_START)
                        pause()

                    def spread(B, bi, q, hn):
                        b0, n = BATCH[bi]
                        pe.wait_ge(s["hot_t_made"], B if bi >= 2 else B - bi + 1)
                        for k in range(n):
                            last = t.matmul(banks[bi % 2][:, k * P:(k + 1) * P],
                                            identb[:, bass.ds(q * HG + b0 + k, 1)].broadcast_to([P, P]),
                                            rdb[:, hn, :], start=True, stop=True)
                        last.then_inc(s["spread"], 1)

                    def pick(B, bi, taken=None):
                        b0, n = BATCH[bi]
                        pe.wait_ge(s["hot_t_made"], B + 2)
                        if bi == 0:
                            pe.wait_ge(s["d_taken"], taken + 1)
                        for k in range(n):
                            tile = pe.snap(tiles[b0 + k], min_val=0, max_val=NT - 1)
                            last = t.matmul(banks[2][:, (b0 + k) * 3:(b0 + k) * 3 + 3], hot_t[:, bi % 2, k * P:(k + 1) * P],
                                            dsplit[:, bass.ds(tile, 1), :], start=True, stop=True)
                        last.then_inc(s["d_picked"], 1)

                    def superblock(l, pr, h, edges):
                        g = l * NSB + 2 * pr + h
                        nxt = (2 * pr + h + 1) * G
                        pe.wait_ge(s["logits_cols"], g + 1)
                        if edges:
                            pe.wait_ge(s["ea_kept"], 2 * (J0 + (2 * pr + h) * EPS_))
                        pause()
                        t.transpose(banks[6][0:G, 0:P], scol[:, :], ident[:, :]).then_inc(s["logits_rows"], 1)
                        pe.wait_ge(s["prefix_max"], g + 1)
                        pause()
                        t.transpose(banks[7][0:1, 0:G], fmax[:, P - 1:P], ident[0:G, 0:G]).then_inc(s["tails_row"], 1)
                        pe.wait_ge(s["carry_row"], g + 1)
                        pause()
                        t.transpose(banks[6][0:G, 0:1], crow[:, h, 0:G], ident[0:1, 0:1]).then_inc(s["carry_cols"], 1)
                        pe.wait_ge(s["suffix_max"], g + 1)
                        pause()
                        t.transpose(banks[7][0:1, 0:G], bmax[:, 0:1], ident[0:G, 0:G]).then_inc(s["heads_row"], 1)
                        pe.wait_ge(s["back_row"], g + 1)
                        pause()
                        t.transpose(banks[6][0:G, 0:1], brow[:, h, 1:G + 1], ident[0:1, 0:1]).then_inc(s["back_cols"], 1)
                        pe.wait_ge(s["w_rows"], g + 1)
                        pe.wait_ge(s["maxima_made"], g + 1)
                        pause()
                        t.transpose(banks[7][:, 0:G], wrow[:, :], ident[0:G, 0:G])
                        t.transpose(banks[7][:, G:2 * G], lastmax[:, :], ident[0:G, 0:G])
                        for k in range(L):
                            last = t.transpose(banks[7][:, (2 + k) * G:(3 + k) * G], tirow[:, h, k * P:(k + 1) * P],
                                               ident[0:G, 0:G])
                        last.then_inc(s["w_cols"], 1)
                        pe.wait_ge(s["w_cols"], g + 1)
                        pe.sem_inc(s["struct_used"], 1)
                        pe.wait_ge(s["carry_factor"], g + 1)
                        t.matmul(banks[6][:, 0:1], ones_row[:, :], drop[:, 1:2], start=True, stop=True)\
                            .then_inc(s["factor_spread"], 1)
                        pe.wait_ge(s["rd_rows"], g + 2)
                        if edges:
                            pe.wait_ge(s["fcol_made"], g + 1)
                        pause()
                        with pe.Fori(0, 2) as q:
                            t.load(tiles, ntile[0:1, bass.ds(nxt + q * HG, HG)])
                            for bi, (b0, n) in enumerate(BATCH):
                                B = l * DLAYER + (2 * pr + h + 1) * DSB + q * NBT + bi
                                spread(B, bi, q, 1 - h)
                                for u in range(b0, b0 + n):
                                    gv = (g * 2 + q) * HG + u
                                    pe.wait_ge(s["hot_made"], gv + 1)
                                    pe.wait_ge(s["weighted"], gv + 1)
                                    if u % 2 == 0:
                                        pe.wait_ge(s["acc_done"], gv + 1 if u == 0 else gv)
                                    t.matmul(visit_sum(u), hot[:, u % 8, :],
                                             ring[:, bass.ds(h * G + q * HG + u, 1), :], start=True, stop=True)\
                                        .then_inc(s["summed"], 1)
                                if bi:
                                    pick(B - 1, bi - 1, l * 2 * (NSB + 1) + (2 * pr + h + 1) * 2 + q)
                                if edges:
                                    j = J0 + (2 * pr + h) * EPS_ + q * (EPS_ // 2) + bi // 2
                                    jp = (J0 + bi // 2) % 2
                                    if bi % 2 == 0:
                                        pe.wait_ge(ea_loaded[jp], 16 * ((2 * pr + h) * (EPS_ // 2) + q * (EPS_ // 4)
                                                                        + (J0 + bi // 2) // 2 + 1))
                                    turn_group(2 * j + bi % 2, jp, bi % 2)
                            B = l * DLAYER + (2 * pr + h + 1) * DSB + q * NBT + NBT - 1
                            pick(B, NBT - 1)

                    pe.sem_inc(s["d_picked"], 1)
                    pe.sem_inc(s["x_turned"], AT_START)
                    pe.sem_inc(s["h_made"], AT_START)
                    transform(0)
                    for j in range(EXTRA + 1):
                        turn_item(j, j % 2, j // 2 + 1)
                    with pe.Fori(0, AHEAD // 2) as i:
                        for k in range(2):
                            j = item_of_tile(0) + k
                            turn_item(j + 2 * i, j % 2, j // 2 + 1 + i)

                    def first_d(l):
                        pe.wait_ge(s["rd_rows"], l * NSB + 1)
                        pause()
                        with pe.Fori(0, 2) as q:
                            t.load(tiles, ntile[0:1, bass.ds(q * HG, HG)])
                            for bi in range(NBT):
                                B = l * DLAYER + q * NBT + bi
                                spread(B, bi, q, 0)
                                if bi:
                                    pick(B - 1, bi - 1, l * 2 * (NSB + 1) + q)
                            pick(l * DLAYER + q * NBT + NBT - 1, NBT - 1)

                    first_d(0)
                    with pe.Fori(0, EPAIRS) as pr:
                        for h in range(2):
                            superblock(0, pr, h, True)
                    t_product(2 * LAST_ITEM + 1, 1)
                    with pe.Fori(EPAIRS, NP2) as pr:
                        for h in range(2):
                            superblock(0, pr, h, False)
                    with pe.Fori(1, L) as l:
                        transform(l)
                        first_d(l)
                        with pe.Fori(0, NP2) as pr:
                            for h in range(2):
                                superblock(l, pr, h, False)

                @block.scalar
                def _(act):
                    a = nc.scalar

                    def keep_turned(c, cpar, p=P):
                        act.wait_ge(s["ea_turned"], c + 1)
                        if not isinstance(c, int) or c >= 2:
                            act.wait_ge(s["t_made"], c - 1)
                        a.activation(eat[:, cpar, 0:SUB * p], banks[6 + cpar][:, 0:SUB * p], ACT.Copy)\
                            .then_inc(s["ea_kept"], 1)

                    def keep_t(c, jpar, gi, stores, p=P):
                        act.wait_ge(s["t_made"], c + 1)
                        if gi == 0:
                            act.wait_ge(t_stored[jpar], 16 * stores)
                        place = tcol[0:p, jpar, :].rearrange("p (l k) -> p k l", l=L)[:, gi * SUB:(gi + 1) * SUB, :]
                        a.activation(place, banks[5][0:p, 0:SUB * L].rearrange("p (k l) -> p k l", l=L), ACT.Copy)\
                            .then_inc(s["t_kept"], 1)

                    def item(j, jpar, half):
                        c = 2 * j
                        rest, after_rest = j is REST_ITEM, j is AFTER_REST
                        p = RP if rest else P
                        keep_turned(c, 0, p)
                        if not rest:
                            keep_t(c - 1, 1 - jpar, 1, None, RP if after_rest else P)
                        keep_turned(c + 1, 1, p)
                        keep_t(c, jpar, 0, half, p)

                    def norm_group(c, done):
                        for k in range(CT):
                            tile = nodes[:, bass.ds(c * CT + k, 1), 0:D]
                            last = a.activation(tile, tile, ACT.Identity, scale=sm[:, 15, bass.ds(c * CT + k, 1)],
                                                bias=sm[:, 13, bass.ds(c * CT + k, 1)])
                        last.then_inc(done, 1)

                    def transform(l):
                        with act.Fori(0, NT // 7) as ti:
                            for u in range(7):
                                n = l * NT + 7 * ti + u
                                act.wait_ge(s["x_turned"], n + 1 + AT_START)
                                act.wait_ge(s["h_made"], reuse(n, u))
                                act.sem_inc(s["act_paused"], 1)
                                if isinstance(l, int):
                                    kept = a.activation(xt[:, u % TB, :], banks[u % TB][:, 0:P], ACT.Copy)
                                else:
                                    kept = a.activation(xt[:, u % TB, :], banks[u % TB][:, 0:P], ACT.Identity,
                                                        scale=gb[:, bass.ds(l - 1, 1), 0], bias=gb[:, bass.ds(l - 1, 1), 1])
                                kept.then_inc(s["x_turned_kept"], 1)

                    def superblock(l, pr, h, edges):
                        g = l * NSB + 2 * pr + h
                        act.wait_ge(s["diff_made"], g + 1)
                        a.activation(wrow[:, :], diff[:, :], ACT.Exp).then_inc(s["w_rows"], 1)
                        act.wait_ge(s["carry_drop"], g + 1)
                        a.activation(drop[:, 1:2], drop[:, 0:1], ACT.Exp).then_inc(s["carry_factor"], 1)
                        act.wait_ge(s["weights_ready"], g + 1)
                        act.sem_inc(s["act_paused"], 1)
                        with act.Fori(0, 2) as q:
                            def weigh(bi):
                                b0, n = BATCH[bi]
                                for u in range(b0, b0 + n):
                                    slot = ring[:, bass.ds(h * G + q * HG + u, 1), 0:D + 1]
                                    a.activation(slot, slot, ACT.Copy, scale=wcol[:, h, bass.ds(q * HG + u, 1)])\
                                        .then_inc(s["weighted"], 1)
                            weigh(0)
                            for bi in range(NBT):
                                if bi + 1 < NBT:
                                    weigh(bi + 1)
                                if edges:
                                    base = (2 * pr + h) * EPS_ + q * (EPS_ // 2)
                                    half = (2 * pr + h) * (EPS_ // 2) + q * (EPS_ // 4) + (J0 + bi // 2) // 2
                                    j = J0 + base + bi // 2
                                    jp = (J0 + bi // 2) % 2
                                    c = 2 * j + bi % 2
                                    keep_turned(c, bi % 2)
                                    if bi % 2 == 0:
                                        keep_t(c - 1, 1 - jp, 1, None)
                                    else:
                                        keep_t(c - 1, jp, 0, half)

                    def loop_over_self(l):
                        act.wait_ge(s["f_made"], l + 1)
                        a.activation(sm[:, 8:10, :], sm[:, 6:8, :], ACT.Exp).then_inc(s["f_exp"], 1)

                    def std(count):
                        act.wait_ge(s["var_made"], count)
                        a.activation(sm[:, 14, :], sm[:, 13, :], ACT.Sqrt).then_inc(s["std_made"], 1)

                    act.sem_inc(s["x_turned_kept"], AT_START)
                    act.wait_ge(s["base_set"], 3)
                    transform(0)
                    for j in range(EXTRA + 1):
                        item(j, j % 2, j // 2)
                    with act.Fori(0, AHEAD // 2) as i:
                        for k in range(2):
                            j = item_of_tile(0) + k
                            item(j + 2 * i, j % 2, j // 2 + i)
                    with act.Fori(0, EPAIRS) as pr:
                        for h in range(2):
                            superblock(0, pr, h, True)
                    keep_t(2 * LAST_ITEM + 1, LAST_ITEM % 2, 1, None)
                    with act.Fori(EPAIRS, NP2) as pr:
                        for h in range(2):
                            superblock(0, pr, h, False)
                    loop_over_self(0)
                    std(1)
                    with act.Fori(1, L) as l:
                        transform(l)
                        with act.Fori(0, NP2) as pr:
                            for h in range(2):
                                superblock(l, pr, h, False)
                        loop_over_self(l)
                        std(l + 1)
                    act.wait_ge(s["nodes_ready"], L)
                    act.sem_inc(s["act_paused"], 1)
                    with act.Fori(0, NCK) as c:
                        norm_group(c, s["y_normed"])
                    std(L + 1)
                    act.wait_ge(s["nodes_ready"], L + 1)
                    act.sem_inc(s["act_paused"], 1)
                    with act.Fori(0, NORM_ACT) as c:
                        norm_group(c, s["out_by_act"])

                @block.vector
                def _(dve):
                    v = nc.vector
                    VR = 4 * (-(-HG // 8))
                    tiles = [dve.alloc_register(f"vtile{k}") for k in range(VR)]
                    SB_LINKS, TOP_LINKS, END_LINKS, GROUP_LINKS = 7, 5, 15, 5
                    PER_LAYER = TOP_LINKS + END_LINKS + NSB * SB_LINKS + NCK * GROUP_LINKS

                    def norm_group(c, done):
                        for k in range(CT):
                            tile = nodes[:, bass.ds(c * CT + k, 1), 0:D]
                            last = v.tensor_scalar(tile, tile, sm[:, 15, bass.ds(c * CT + k, 1)],
                                                   sm[:, 13, bass.ds(c * CT + k, 1)], ALU.mult, ALU.add)
                        last.then_inc(done, 1)

                    def statistics(link, c):
                        dve.sem_inc(s["dve_paused"], 1)
                        for k in range(CT):
                            last = v.bn_stats(stats[:, k, :], nodes[:, bass.ds(c * CT + k, 1), 0:D])
                        link(last)
                        dve.sem_inc(s["dve_paused"], 1)
                        for k in range(CT):
                            last = v.bn_aggr(mvg[:, k, :], stats[:, k, :])
                        link(last)
                        link(v.tensor_copy(mv[:, bass.ds(c * CT, CT), :], mvg[:, :, :]))

                    def norm_scales(count, link):
                        v.tensor_scalar(sm[:, 13, :], mv[:, :, 1], LN_EPS, None, ALU.add).then_inc(s["var_made"], 1)
                        dve.wait_ge(s["std_made"], count)
                        link(v.reciprocal(sm[:, 15, :], sm[:, 14, :]))
                        v.scalar_tensor_tensor(sm[:, 13, :], mv[:, :, 0], -1.0, sm[:, 15, :], ALU.mult, ALU.mult)\
                            .then_inc(s["nodes_ready"], 1)

                    def turn_hot(B, bi):
                        n = BATCH[bi][1]
                        dve.wait_ge(s["spread"], B + 1)
                        dve.wait_ge(s["d_picked"], B if bi >= 2 else B - bi + 1)
                        v.tensor_scalar(hot_t[:, bi % 2, 0:n * P], banks[bi % 2][:, 0:n * P],
                                        iota_col[:, :], None, ALU.is_equal).then_inc(s["hot_t_made"], 1)

                    def take_d(B_end, q, hn):
                        dve.wait_ge(s["d_picked"], B_end + 1)
                        v.tensor_reduce(dedge[:, hn, bass.ds(q * HG, HG)],
                                        banks[2][:, 0:3 * HG].rearrange("p (v c) -> p v c", c=3),
                                        AX.X, ALU.add).then_inc(s["d_taken"], 1)

                    def stage_index(m_sb, h):
                        v.tensor_copy(ixs[:, h, :], idx[:, bass.ds(m_sb * G, G)]).then_inc(s["index_staged"], 1)

                    def stage_chunk(m_sb, h):
                        v.tensor_copy(cvs[:, h:h + 1], cvi[:, bass.ds(m_sb, 1)]).then_inc(s["chunk_staged"], 1)

                    def layer_start(l):
                        def keep_h(ti):
                            for u in range(7):
                                dve.wait_ge(s["h_made"], l * NT + 7 * ti + u + 1 + AT_START)
                                v.tensor_copy(hbuf[:, bass.ds(7 * ti + u, 1), :], banks[TB + u % TB][:, 0:ROW])
                                v.tensor_copy(dnode[:, bass.ds(7 * ti + u, 1)], banks[TB + u % TB][:, D + 2:D + 3])\
                                    .then_inc(s["h_kept"], 1)
                        if isinstance(l, int):
                            with dve.Fori(0, NCK) as ti:
                                keep_h(ti)
                        else:
                            dve.wait_ge(s["nodes_ready"], l)
                            dve.sem_inc(s["dve_paused"], 1)
                            norm_group(0, s["x_normed"])
                            with dve.Fori(0, NCK - 1) as ti:
                                norm_group(ti + 1, s["x_normed"])
                                keep_h(ti)
                            keep_h(NCK - 1)
                        dve.wait_ge(s["h_kept"], (l + 1) * NT + AT_START)
                        v.memset(hbuf[:, :, C_ONE], 1.0).then_inc(s["h_ready"], 1)
                        link = Chain(dve, s["dve_links"], l * PER_LAYER)
                        v.memset(crow[:, 1, G:G + 1], -BIG)
                        link(v.tensor_copy(dsplit[:, :, 0], dnode[:, :]))
                        link(v.tensor_tensor(drest[:, 0, :], dnode[:, :], dsplit[:, :, 0], ALU.subtract))
                        link(v.tensor_copy(dsplit[:, :, 1], drest[:, 0, :]))
                        link(v.tensor_tensor(drest[:, 1, :], drest[:, 0, :], dsplit[:, :, 1], ALU.subtract))
                        link(v.tensor_copy(dsplit[:, :, 2], drest[:, 1, :]))
                        assert link.n == TOP_LINKS
                        dve.wait_ge(s["nodes_cleared"], l + 1)
                        dve.sem_inc(s["dve_paused"], 1)
                        with dve.Fori(0, 2) as q:
                            for bi in range(NBT):
                                turn_hot(l * DLAYER + q * NBT + bi, bi)
                            take_d(l * DLAYER + (q + 1) * NBT, q, 0)

                    def superblock(l, pr, h, fresh):
                        g = l * NSB + 2 * pr + h
                        pair = l * NP2 + pr + 1
                        first = (2 * pr + h) * G
                        link = Chain(dve, s["dve_links"], l * PER_LAYER + TOP_LINKS + (2 * pr + h) * SB_LINKS)
                        field = {f: strow[:, h, f * P:(f + 1) * P] for f in range(NFIELD)}
                        link(v.tensor_copy(crow[:, h, 0:1], crow[:, 1 - h, G:G + 1]))
                        dve.wait_ge(struct_loaded[1 - h], 48 * (pair + h))
                        v.tensor_copy(rdb[0:G, 1 - h, :], strow[:, 1 - h, S_RD * P:(S_RD + 1) * P]).then_inc(s["rd_rows"], 1)
                        if fresh:
                            v.tensor_scalar(outside[:, :], field[S_RD], 0.0, -BIG, ALU.is_lt, ALU.mult)\
                                .then_inc(s["outside_made"], 1)
                            dve.wait_ge(s["outside_made"], g + 1)
                        dve.wait_ge(s["d_taken"], l * 2 * (NSB + 1) + (2 * pr + h + 1) * 2 + 1)
                        dve.wait_ge(gathered[h], 16 * G * pair)
                        stage_index(2 * pr + h + 2, h)
                        v.tensor_tensor(scol[:, :], ring[:, h * G:(h + 1) * G, C_S], dedge[:, h, :], ALU.add)\
                            .then_inc(s["logits_cols"], 1)
                        if fresh:
                            dve.wait_ge(t_gathered[h], 16 * pair)
                            dve.wait_ge(ti_stored[h], 16 * pr + 1)
                            for k in range(L):
                                v.tensor_tensor(tirow[:, h, k * P:(k + 1) * P].rearrange("g (a b) -> g a b", b=KE),
                                                traw[:, h, :].rearrange("g (a l b) -> g l a b", l=L, b=KE)[:, k],
                                                outside[:, :].rearrange("g (a b) -> g a b", b=KE), ALU.add)\
                                    .then_inc(s["t_masked"], 1)
                            dve.wait_ge(s["t_masked"], L * (g + 1))
                            stage_chunk(2 * pr + h + 2, h)
                            t_row = tirow[:, h, 0:P]
                        else:
                            dve.wait_ge(ti_loaded[h], 16 * (pair - NP2))
                            t_row = tirow[:, h, bass.ds(l * P, P)]
                        dve.wait_ge(s["logits_rows"], g + 1)
                        link(v.tensor_tensor(logit_u[:, :], banks[6][0:G, 0:P], t_row, ALU.add))
                        link(v.scalar_tensor_tensor(logit[:, :], logit_u[:, :], SLOPE, logit_u[:, :], ALU.mult, ALU.max))
                        v.tensor_tensor_scan(fmax[:, :], field[S_RF], logit[:, :], -BIG, ALU.add, ALU.max)\
                            .then_inc(s["prefix_max"], 1)
                        dve.wait_ge(s["tails_row"], g + 1)
                        v.tensor_tensor_scan(crow[:, h, 1:G + 1], flags[:, h, 0, :], banks[7][0:1, 0:G],
                                             crow[:, h, 0:1], ALU.add, ALU.max).then_inc(s["carry_row"], 1)
                        dve.wait_ge(s["carry_cols"], g + 1)
                        link(v.scalar_tensor_tensor(fmax2[:, :], field[S_OF], banks[6][0:G, 0:1], fmax[:, :],
                                                    ALU.add, ALU.max))
                        v.tensor_tensor_scan(bmax[:, ::-1], field[S_RB][:, ::-1], fmax2[:, ::-1], -BIG,
                                             ALU.add, ALU.max).then_inc(s["suffix_max"], 1)
                        dve.wait_ge(s["heads_row"], g + 1)
                        v.tensor_tensor_scan(brow[:, h, 0:G][:, ::-1], flags[:, h, 1, :][:, ::-1],
                                             banks[7][0:1, 0:G][:, ::-1], -BIG, ALU.add, ALU.max)\
                            .then_inc(s["back_row"], 1)
                        dve.wait_ge(s["back_cols"], g + 1)
                        link(v.scalar_tensor_tensor(segmax[:, :], field[S_OB], banks[6][0:G, 0:1], bmax[:, :],
                                                    ALU.add, ALU.max))
                        v.tensor_tensor(diff[:, :], logit[:, :], segmax[:, :], ALU.subtract).then_inc(s["diff_made"], 1)
                        v.scalar_tensor_tensor(lastmax[:, :], field[S_RB], -1.0 / BIG, segmax[:, :],
                                               ALU.mult, ALU.mult).then_inc(s["maxima_made"], 1)
                        dve.wait_ge(s["back_row"], g + 1)
                        link(v.tensor_tensor(drop[:, 0:1], crow[:, h, 0:1], brow[:, h, 0:1], ALU.subtract))
                        v.tensor_scalar(drop[:, 0:1], drop[:, 0:1], 0.0, None, ALU.min).then_inc(s["carry_drop"], 1)
                        v.load(tiles[0:1], ntile[0:1, bass.ds(first, 1)])
                        dve.wait_ge(s["w_cols"], g + 1)
                        v.tensor_copy(wcol[:, h, :], banks[7][:, 0:G])
                        v.tensor_copy(ring[:, h * G:(h + 1) * G, C_M:C_T + L].rearrange("p v c -> p c v"),
                                      banks[7][:, G:(2 + L) * G].rearrange("p (c v) -> p c v", c=1 + L))\
                            .then_inc(s["weights_ready"], 1)
                        dve.wait_ge(s["factor_spread"], g + 1)
                        v.scalar_tensor_tensor(fcol[:, :], carry_hot[:, bass.ds(2 * pr + h, 1)], banks[6][:, 0:1],
                                               carry_not[:, bass.ds(2 * pr + h, 1)], ALU.mult, ALU.add)\
                            .then_inc(s["fcol_made"], 1)
                        dve.wait_ge(s["fcol_made"], g + 1)
                        dve.wait_ge(s["acc_done"], g * G + 2)
                        tile = dve.snap(tiles[0], min_val=0, max_val=NT - 1)
                        own = nodes[:, bass.ds(tile, 1), 0:D + 1]
                        link(v.tensor_scalar(own, own, fcol[:, :], None, ALU.mult))
                        assert link.n == SB_LINKS, link.n
                        dve.sem_inc(s["dve_paused"], 1)

                        with dve.Fori(0, 2) as q:
                            def accumulate(u):
                                if u % VR == 0:
                                    some = min(VR, HG - u)
                                    v.load(tiles[0:some], ntile[0:1, bass.ds(first + q * HG + u, some)])
                                gv = (g * 2 + q) * HG + u
                                if u % 2 == 0:
                                    dve.wait_ge(s["summed"], gv + min(2, HG - u))
                                dve.wait_ge(s["acc_done"], gv + 2)
                                tile = dve.snap(tiles[u % VR], min_val=0, max_val=NT - 1)
                                own = nodes[:, bass.ds(tile, 1), :]
                                v.tensor_tensor(own, own, visit_sum(u), ALU.add)\
                                    .then_inc(s["acc_done"], 1)

                            def one_hot(u):
                                v.tensor_scalar(hot[:, u % 8, :], iota_row[:, :],
                                                rdcol[:, bass.ds(first + q * HG + u, 1)], None, ALU.is_equal)\
                                    .then_inc(s["hot_made"], 1)
                            for u in range(LEAD):
                                one_hot(u)
                            for bi, (b0, n) in enumerate(BATCH):
                                for u in range(b0, b0 + n):
                                    if u + LEAD < HG:
                                        one_hot(u + LEAD)
                                    if u >= 2:
                                        accumulate(u - 2)
                                turn_hot(l * DLAYER + (2 * pr + h + 1) * DSB + q * NBT + bi, bi)
                            accumulate(HG - 2)
                            accumulate(HG - 1)
                            dve.sem_inc(s["slots_free"], 1)
                            take_d(l * DLAYER + (2 * pr + h + 1) * DSB + (q + 1) * NBT, q, 1 - h)

                    def layer_end(l):
                        link = Chain(dve, s["dve_links"], l * PER_LAYER + TOP_LINKS + NSB * SB_LINKS)
                        dve.wait_ge(s["acc_done"], (l + 1) * NV + 2)
                        cnt = nodes[:, :, C_CNT]
                        tsum = nodes[:, :, bass.ds(C_T + l, 1)].rearrange("p t o -> p (t o)")
                        link(v.tensor_scalar(sm[:, 0, :], cnt, 1.0, None, ALU.max))
                        link(v.reciprocal(sm[:, 1, :], sm[:, 0, :]))
                        link(v.tensor_tensor(sm[:, 2, :], tsum, sm[:, 1, :], ALU.mult))
                        link(v.tensor_tensor(sm[:, 2, :], sm[:, 2, :], hbuf[:, :, C_S], ALU.add))
                        link(v.tensor_tensor(sm[:, 2, :], sm[:, 2, :], dnode[:, :], ALU.add))
                        link(v.scalar_tensor_tensor(sm[:, 3, :], sm[:, 2, :], SLOPE, sm[:, 2, :], ALU.mult, ALU.max))
                        link(v.tensor_scalar(sm[:, 4, :], cnt, 0.0, -BIG, ALU.is_equal, ALU.mult))
                        link(v.tensor_tensor(sm[:, 4, :], sm[:, 4, :], nodes[:, :, C_M], ALU.add))
                        link(v.tensor_tensor(sm[:, 5, :], sm[:, 4, :], sm[:, 3, :], ALU.max))
                        link(v.tensor_tensor(sm[:, 6, :], sm[:, 4, :], sm[:, 5, :], ALU.subtract))
                        v.tensor_tensor(sm[:, 7, :], sm[:, 3, :], sm[:, 5, :], ALU.subtract).then_inc(s["f_made"], 1)
                        dve.wait_ge(s["f_exp"], l + 1)
                        link(v.tensor_tensor(sm[:, 10, :], nodes[:, :, C_ONE], sm[:, 8, :], ALU.mult))
                        link(v.tensor_tensor(sm[:, 10, :], sm[:, 10, :], sm[:, 9, :], ALU.add))
                        link(v.reciprocal(sm[:, 11, :], sm[:, 10, :]))
                        v.tensor_tensor(sm[:, 12, :], sm[:, 9, :], sm[:, 11, :], ALU.mult).then_inc(s["c_made"], 1)
                        link(v.tensor_tensor(sm[:, 11, :], sm[:, 8, :], sm[:, 11, :], ALU.mult))
                        assert link.n == END_LINKS - 1, link.n
                        dve.sem_inc(s["dve_paused"], 1)
                        base = link.base + link.n
                        with dve.Fori(0, NCK) as c:
                            link = Chain(dve, s["dve_links"], base + c * GROUP_LINKS)
                            own = group(nodes, c)
                            link(v.tensor_tensor(own, own, bc_group(sm[:, 11, :], c), ALU.mult))
                            dve.wait_ge(s["h_scaled"], l * NCK + c + 1)
                            link(v.tensor_tensor(own, own, group(hbuf, c), ALU.add))
                            statistics(link, c)
                            assert link.n == GROUP_LINKS
                        norm_scales(l + 1, Chain(dve, s["dve_links"], base + NCK * GROUP_LINKS))

                    dve.sem_inc(s["slots_free"], 4)
                    dve.sem_inc(s["acc_done"], 2)
                    dve.sem_inc(s["h_kept"], AT_START)
                    dve.sem_inc(s["hot_t_made"], 1)
                    dve.sem_inc(s["d_taken"], 1)
                    v.memset(rdb[:, :, :], 0.0).then_inc(s["base_set"], 1)
                    v.memset(ring[:, :, C_CNT], 1.0).then_inc(s["base_set"], 1)
                    v.memset(brow[:, :, G:G + 1], -BIG).then_inc(s["base_set"], 1)
                    for h in range(2):
                        stage_index(h, h)
                        stage_chunk(h, h)
                    dve.wait_ge(s["base_set"], 3)
                    dve.wait_ge(struct_loaded[0], 48)
                    v.tensor_copy(rdb[0:G, 0, :], strow[:, 0, S_RD * P:(S_RD + 1) * P]).then_inc(s["rd_rows"], 1)
                    layer_start(0)
                    with dve.Fori(0, NP2) as pr:
                        for h in range(2):
                            superblock(0, pr, h, True)
                    layer_end(0)
                    with dve.Fori(1, L) as l:
                        layer_start(l)
                        with dve.Fori(0, NP2) as pr:
                            for h in range(2):
                                superblock(l, pr, h, False)
                        layer_end(l)
                    dve.sem_inc(s["dve_paused"], 1)
                    with dve.Fori(0, NCK) as c:
                        link = Chain(dve, s["dve_links"], L * PER_LAYER + c * GROUP_LINKS)
                        own = group(nodes, c)
                        dve.wait_ge(s["y_normed"], c + 1)
                        link(v.tensor_tensor(own, own, bc_param(L - 1, 1), ALU.mult))
                        dve.wait_ge(s["x_beta"], c + 1)
                        link(v.tensor_tensor(own, own, group(xagain, c), ALU.add))
                        statistics(link, c)
                    norm_scales(L + 1, Chain(dve, s["dve_links"], L * PER_LAYER + NCK * GROUP_LINKS))
                    dve.wait_ge(s["nodes_ready"], L + 1)
                    dve.sem_inc(s["dve_paused"], 1)
                    with dve.Fori(NORM_ACT, NCK) as c:
                        norm_group(c, s["out_by_dve"])


def kernel(x, src, dst, edge_attr_128, L0_gnn_W, L0_gnn_att_src, L0_gnn_att_dst, L0_gnn_W_e,
           L0_gnn_att_edge, L0_gnn_bias, L0_gnn_ln_gamma, L0_gnn_ln_beta):
    import concourse.bacc as bacc
    from concourse.bass_utils import run_bass_kernel_spmd as run

    xp = np.zeros((NT * P, D), np.float32)
    xp[:N] = np.asarray(x)
    d = np.full(NCH * P + 2, 1 << 20, np.int32)
    d[0] = -1
    d[1:E + 1] = np.asarray(dst)
    s = np.zeros(NCH * P, np.int32)
    s[:E] = np.asarray(src)
    ei = np.empty((NCH, EIW), np.int32)
    for k in range(P + 2):
        ei[:, k] = d[k:k + (NCH - 1) * P + 1:P]
    ei[:, P + 2:] = s.reshape(NCH, P)
    last = np.full(NCH, N - 1, np.int32)
    last[:NCH - 1] = np.asarray(dst)[P - 1::P][:NCH - 1]
    att = np.empty((D, 5 * L), np.float32)
    for l in range(L):
        att[:, 3 * l] = np.asarray(L0_gnn_att_src)[l]
        att[:, 3 * l + 1] = np.asarray(L0_gnn_att_dst)[l]
        att[:, 3 * l + 2] = np.asarray(L0_gnn_att_edge)[l]
        att[:, 3 * L + 2 * l] = np.asarray(L0_gnn_ln_gamma)[l]
        att[:, 3 * L + 2 * l + 1] = np.asarray(L0_gnn_ln_beta)[l]
    par = np.stack([np.asarray(L0_gnn_bias), np.asarray(L0_gnn_ln_gamma), np.asarray(L0_gnn_ln_beta)], 1).reshape(-1)
    w = np.asarray(L0_gnn_W)
    arrays = {
        "x": xp, "ei": ei, "chunk_last": last, "edge_attr": np.ascontiguousarray(edge_attr_128),
        "w": np.ascontiguousarray(w), "wt": np.ascontiguousarray(w.transpose(0, 2, 1)),
        "wet": np.ascontiguousarray(np.asarray(L0_gnn_W_e).transpose(0, 2, 1)), "att": att, "params": par,
    }
    nc = bacc.Bacc("TRN2", target_bir_lowering=False, num_devices=1)
    args = [nc.dram_tensor(f"in_{n}", a.shape, mybir.dt.from_np(a.dtype), kind="ExternalInput").ap()
            for n, a in arrays.items()]
    args.append(nc.dram_tensor("out_0", (N, D), FP32, kind="ExternalOutput").ap())
    build(nc, *args)
    r = run(nc, [{f"in_{n}": a for n, a in arrays.items()}], core_ids=[0])
    return r.results[0]["out_0"]
```
